# Optimizing a Trainium2 kernel written in Bass

```python
import numpy as np
import jax
import jax.numpy as jnp

def _softmax(x, axis=-1):
    return jax.nn.softmax(x, axis=axis)

def _gelu(x):
    return jax.nn.gelu(x, approximate=True)

def _silu(x):
    return jax.nn.silu(x)

def _sigmoid(x):
    return jax.nn.sigmoid(x)

def _layernorm(x, axis=-1, eps=1e-05):
    m = jnp.mean(x, axis=axis, keepdims=True)
    v = jnp.var(x, axis=axis, keepdims=True)
    return (x - m) / jnp.sqrt(v + eps)

def _scatter_add(tgt, idx, src, axis=0):
    return tgt.at[idx].add(src)

def _segment_sum(src, seg, n):
    return jax.ops.segment_sum(src, seg, n)
kernel_name = 'mk_xattn_seq_d4_seqx_r8_54000a'

def setup_inputs(seed: int=0):
    np.random.seed(seed)
    _w = jnp.asarray

    def _rec_inputs():
        import jax
        import jax.numpy as jnp
        _rk = jax.random.key(seed)
        x = -7.109e-05 + 0.9999 * jax.random.normal(jax.random.fold_in(_rk, 1), (2, 512, 128), jnp.float32)
        _lenS = 512 - jax.random.randint(jax.random.fold_in(_rk, 7), (2,), 0, max(1, 512 // 4) + 1, jnp.int32)
        _lenS2 = 77 - jax.random.randint(jax.random.fold_in(_rk, 8), (2,), 0, max(1, 77 // 4) + 1, jnp.int32)
        _ctx_1024P = jax.random.normal(jax.random.fold_in(_rk, 11), (2, 16, 128), jnp.float32)
        _ctx_1024c = jax.random.dirichlet(jax.random.fold_in(_rk, 511), 0.3 * jnp.ones((16,), jnp.float32), (2, 77))
        _ctx_1024t = jnp.einsum('bsk,bkd->bsd', _ctx_1024c, _ctx_1024P)
        _ctx_1024t = _ctx_1024t * jax.lax.rsqrt(jnp.mean(jnp.square(_ctx_1024t)) + 1e-12) * 0.953939
        ctx_1024 = -5.72187e-05 + 0.999849 * (_ctx_1024t + 0.3 * jax.random.normal(jax.random.fold_in(_rk, 611), (2, 77, 128), jnp.float32))
        return (x, ctx_1024)
    x, ctx_1024 = _rec_inputs()

    def _L0_xattn_setup():
        import jax, jax.numpy as jnp
        import numpy as np
        TOPK = 10
        NUM_HEADS = 16
        key = jax.random.key(seed)
        ks = jax.random.split(key, 8)
        B, N, S, D = (32, 256, 256, 128)
        sc = 1.0 / np.sqrt(D)
        return {'base_hidden': jax.random.normal(ks[0], (B, N, D), jnp.float32), 'scaffold_hidden': jax.random.normal(ks[1], (B, S, D), jnp.float32), 'in_proj_w': jax.random.normal(ks[2], (3 * D, D), jnp.float32) * sc, 'in_proj_b': jax.random.normal(ks[3], (3 * D,), jnp.float32) * 0.02, 'out_w': jax.random.normal(ks[4], (D, D), jnp.float32) * sc, 'out_b': jax.random.normal(ks[5], (D,), jnp.float32) * 0.02, 'score_w': jax.random.normal(ks[6], (1, D), jnp.float32) * sc, 'score_b': jax.random.normal(ks[7], (1,), jnp.float32) * 0.02}
    _L0_xattn_all = _L0_xattn_setup()
    _L0_xattn_in = {k: v for k, v in _L0_xattn_all.items() if k in ('in_proj_w', 'in_proj_b', 'out_w', 'out_b', 'score_w', 'score_b')}
    del _L0_xattn_all

    def _L1_xattn_setup():
        import jax, jax.numpy as jnp
        import numpy as np
        D_MODEL = 128
        D_FF = 512
        EPS = 1e-05

        def layer_norm(x, gamma, beta):
            mu = jnp.mean(x, axis=-1, keepdims=True)
            var = jnp.var(x, axis=-1, keepdims=True)
            return (x - mu) * jax.lax.rsqrt(var + EPS) * gamma + beta

        def attention(x_q, x_kv, WQ, WK, WV, causal):
            Q = x_q @ WQ
            K = x_kv @ WK
            V = x_kv @ WV
            scale = 1.0 / jnp.sqrt(jnp.asarray(Q.shape[-1], Q.dtype))
            scores = jnp.einsum('bqd,bkd->bqk', Q, K) * scale
            if causal:
                Sq, Sk = (scores.shape[-2], scores.shape[-1])
                mask = jnp.triu(jnp.full((Sq, Sk), -jnp.inf, scores.dtype), k=1)
                scores = scores + mask
            attn = jax.nn.softmax(scores, axis=-1)
            return jnp.einsum('bqk,bkd->bqd', attn, V)
        key = jax.random.key(seed)
        ks = jax.random.split(key, 16)
        B, S = (4, 256)
        s = 0.02
        inp = {'y': jax.random.normal(ks[0], (B, S, D_MODEL), jnp.float32), 'Z': jax.random.normal(ks[1], (B, S, D_MODEL), jnp.float32), 'WQ1': jax.random.normal(ks[2], (D_MODEL, D_MODEL), jnp.float32) * s, 'WK1': jax.random.normal(ks[3], (D_MODEL, D_MODEL), jnp.float32) * s, 'WV1': jax.random.normal(ks[4], (D_MODEL, D_MODEL), jnp.float32) * s, 'WQ2': jax.random.normal(ks[5], (D_MODEL, D_MODEL), jnp.float32) * s, 'WK2': jax.random.normal(ks[6], (D_MODEL, D_MODEL), jnp.float32) * s, 'WV2': jax.random.normal(ks[7], (D_MODEL, D_MODEL), jnp.float32) * s, 'W_ff1': jax.random.normal(ks[8], (D_MODEL, D_FF), jnp.float32) * s, 'b_ff1': jnp.zeros((D_FF,), jnp.float32), 'W_ff2': jax.random.normal(ks[9], (D_FF, D_MODEL), jnp.float32) * s, 'b_ff2': jnp.zeros((D_MODEL,), jnp.float32), 'g1': jnp.ones((D_MODEL,), jnp.float32), 'be1': jnp.zeros((D_MODEL,), jnp.float32), 'g2': jnp.ones((D_MODEL,), jnp.float32), 'be2': jnp.zeros((D_MODEL,), jnp.float32), 'g3': jnp.ones((D_MODEL,), jnp.float32), 'be3': jnp.zeros((D_MODEL,), jnp.float32)}
        return inp
    _L1_xattn_all = _L1_xattn_setup()
    _L1_xattn_in = {k: v for k, v in _L1_xattn_all.items() if k in ('WQ1', 'WK1', 'WV1', 'WQ2', 'WK2', 'WV2', 'W_ff1', 'b_ff1', 'W_ff2', 'b_ff2', 'g1', 'be1', 'g2', 'be2', 'g3', 'be3')}
    del _L1_xattn_all

    def _L2_xattn_setup():
        import jax, jax.numpy as jnp
        import numpy as np
        B, LX, LY = (2, 256, 256)
        E, H = (128, 16)
        HD = E // H
        FF = 512
        EPS = 1e-05

        def _rope_tables(L, d):
            inv = 1.0 / 10000.0 ** (jnp.arange(0, d, 2, dtype=jnp.float32) / d)
            t = jnp.arange(L, dtype=jnp.float32)
            f = jnp.outer(t, inv)
            return (jnp.cos(f), jnp.sin(f))

        def _apply_rope(x, cos, sin):
            d2 = x.shape[-1] // 2
            x1, x2 = (x[..., :d2], x[..., d2:])
            c = cos[None, :, None, :]
            s = sin[None, :, None, :]
            return jnp.concatenate([x1 * c - x2 * s, x2 * c + x1 * s], axis=-1)

        def _ln(x, g, b):
            m = jnp.mean(x, axis=-1, keepdims=True)
            v = jnp.var(x, axis=-1, keepdims=True)
            return (x - m) / jnp.sqrt(v + EPS) * g + b

        def _attn(q, k, v, causal):
            s = jnp.einsum('blhd,bmhd->bhlm', q, k)
            if causal:
                Lq, Lk = (s.shape[2], s.shape[3])
                mask = jnp.tril(jnp.ones((Lq, Lk), dtype=bool))
                s = jnp.where(mask, s, -jnp.inf)
            p = jax.nn.softmax(s, axis=-1)
            return jnp.einsum('bhlm,bmhd->blhd', p, v)

        def _forward(x, y, ln1_g, ln1_b, sa_wq, sa_bq, sa_wk, sa_bk, sa_wv, sa_bv, sa_wo, sa_bo, ln2_g, ln2_b, ca_wq, ca_bq, ca_wk, ca_bk, ca_wv, ca_bv, ca_wo, ca_bo, ln3_g, ln3_b, fc1_w, fc1_b, fc2_w, fc2_b):
            Bx, Lx, _ = x.shape
            Ly = y.shape[1]
            cos, sin = _rope_tables(max(Lx, Ly), HD)
            scale = HD ** (-0.5)
            h = _ln(x, ln1_g, ln1_b)
            q = (h @ sa_wq + sa_bq).reshape(Bx, Lx, H, HD) * scale
            k = (h @ sa_wk + sa_bk).reshape(Bx, Lx, H, HD)
            v = (h @ sa_wv + sa_bv).reshape(Bx, Lx, H, HD)
            q = _apply_rope(q, cos[:Lx], sin[:Lx])
            k = _apply_rope(k, cos[:Lx], sin[:Lx])
            a = _attn(q, k, v, causal=True).reshape(Bx, Lx, E)
            x = x + (a @ sa_wo + sa_bo)
            h = _ln(x, ln2_g, ln2_b)
            q = (h @ ca_wq + ca_bq).reshape(Bx, Lx, H, HD) * scale
            k = (y @ ca_wk + ca_bk).reshape(Bx, Ly, H, HD)
            v = (y @ ca_wv + ca_bv).reshape(Bx, Ly, H, HD)
            q = _apply_rope(q, cos[:Lx], sin[:Lx])
            k = _apply_rope(k, cos[:Ly], sin[:Ly])
            a = _attn(q, k, v, causal=False).reshape(Bx, Lx, E)
            x = x + (a @ ca_wo + ca_bo)
            h = _ln(x, ln3_g, ln3_b)
            return x + (jax.nn.gelu(h @ fc1_w + fc1_b) @ fc2_w + fc2_b)
        key = jax.random.key(seed)
        ks = jax.random.split(key, 16)

        def w(k, *s):
            return jax.random.normal(k, s, jnp.float32) * 0.02
        z = lambda *s: jnp.zeros(s, jnp.float32)
        o = lambda *s: jnp.ones(s, jnp.float32)
        return {'x': jax.random.normal(ks[0], (B, LX, E), jnp.float32), 'y': jax.random.normal(ks[1], (B, LY, E), jnp.float32), 'ln1_g': o(E), 'ln1_b': z(E), 'sa_wq': w(ks[2], E, E), 'sa_bq': z(E), 'sa_wk': w(ks[3], E, E), 'sa_bk': z(E), 'sa_wv': w(ks[4], E, E), 'sa_bv': z(E), 'sa_wo': w(ks[5], E, E), 'sa_bo': z(E), 'ln2_g': o(E), 'ln2_b': z(E), 'ca_wq': w(ks[6], E, E), 'ca_bq': z(E), 'ca_wk': w(ks[7], E, E), 'ca_bk': z(E), 'ca_wv': w(ks[8], E, E), 'ca_bv': z(E), 'ca_wo': w(ks[9], E, E), 'ca_bo': z(E), 'ln3_g': o(E), 'ln3_b': z(E), 'fc1_w': w(ks[10], E, FF), 'fc1_b': z(FF), 'fc2_w': w(ks[11], FF, E), 'fc2_b': z(E)}
    _L2_xattn_all = _L2_xattn_setup()
    _L2_xattn_in = {k: v for k, v in _L2_xattn_all.items() if k in ('ln1_g', 'ln1_b', 'sa_wq', 'sa_bq', 'sa_wk', 'sa_bk', 'sa_wv', 'sa_bv', 'sa_wo', 'sa_bo', 'ln2_g', 'ln2_b', 'ca_wq', 'ca_bq', 'ca_wk', 'ca_bk', 'ca_wv', 'ca_bv', 'ca_wo', 'ca_bo', 'ln3_g', 'ln3_b', 'fc1_w', 'fc1_b', 'fc2_w', 'fc2_b')}
    del _L2_xattn_all

    def _L3_xattn_setup():
        import jax, jax.numpy as jnp
        import numpy as np
        B, N, M, D, H = (2, 256, 77, 128, 16)
        DH = D // H
        SCALE = DH ** (-0.5)
        EPS = 1e-05

        def _round_ste(x):
            return x + jax.lax.stop_gradient(jnp.round(x) - x)

        def _fq(x, delta, zp, n_bits):
            xi = _round_ste(x / delta) + zp
            xq = jnp.clip(xi, 0.0, 2.0 ** n_bits - 1.0)
            return (xq - zp) * delta

        def _ln(x, g, b):
            mu = jnp.mean(x, -1, keepdims=True)
            var = jnp.var(x, -1, keepdims=True)
            return (x - mu) * jax.lax.rsqrt(var + EPS) * g + b

        def _attn(x, ctx, wq, wk, wv, wo, bo, dq, dk, dv, dw):
            b, n, _ = x.shape
            m = ctx.shape[1]
            q = (x @ wq).reshape(b, n, H, DH).transpose(0, 2, 1, 3)
            k = (ctx @ wk).reshape(b, m, H, DH).transpose(0, 2, 1, 3)
            v = (ctx @ wv).reshape(b, m, H, DH).transpose(0, 2, 1, 3)
            sim = jnp.einsum('bhid,bhjd->bhij', _fq(q, dq, 128.0, 8), _fq(k, dk, 128.0, 8)) * SCALE
            attn = jax.nn.softmax(sim, axis=-1)
            out = jnp.einsum('bhij,bhjd->bhid', _fq(attn, dw, 0.0, 8), _fq(v, dv, 128.0, 8))
            out = out.transpose(0, 2, 1, 3).reshape(b, n, D)
            return out @ wo + bo
        key = jax.random.key(seed)
        ks = jax.random.split(key, 16)
        w = lambda k, s: jax.random.normal(k, s, jnp.float32) * 0.02
        d = lambda v: jnp.full((1,), v, jnp.float32)
        return {'x': jax.random.normal(ks[0], (B, N, D), jnp.float32), 'context': jax.random.normal(ks[1], (B, M, D), jnp.float32), 'ln1_g': jnp.ones((D,), jnp.float32), 'ln1_b': jnp.zeros((D,), jnp.float32), 'ln2_g': jnp.ones((D,), jnp.float32), 'ln2_b': jnp.zeros((D,), jnp.float32), 'ln3_g': jnp.ones((D,), jnp.float32), 'ln3_b': jnp.zeros((D,), jnp.float32), 'a1_wq': w(ks[2], (D, D)), 'a1_wk': w(ks[3], (D, D)), 'a1_wv': w(ks[4], (D, D)), 'a1_wo': w(ks[5], (D, D)), 'a1_bo': jnp.zeros((D,), jnp.float32), 'a2_wq': w(ks[6], (D, D)), 'a2_wk': w(ks[7], (D, D)), 'a2_wv': w(ks[8], (D, D)), 'a2_wo': w(ks[9], (D, D)), 'a2_bo': jnp.zeros((D,), jnp.float32), 'ff_w1': w(ks[10], (D, 8 * D)), 'ff_b1': jnp.zeros((8 * D,), jnp.float32), 'ff_w2': w(ks[11], (4 * D, D)), 'ff_b2': jnp.zeros((D,), jnp.float32), 'd_q1': d(0.02), 'd_k1': d(0.02), 'd_v1': d(0.02), 'd_w1': d(1.0 / 255.0), 'd_q2': d(0.02), 'd_k2': d(0.02), 'd_v2': d(0.02), 'd_w2': d(1.0 / 255.0)}
    _L3_xattn_all = _L3_xattn_setup()
    _L3_xattn_in = {k: v for k, v in _L3_xattn_all.items() if k in ('ln1_g', 'ln1_b', 'ln2_g', 'ln2_b', 'ln3_g', 'ln3_b', 'a1_wq', 'a1_wk', 'a1_wv', 'a1_wo', 'a1_bo', 'a2_wq', 'a2_wk', 'a2_wv', 'a2_wo', 'a2_bo', 'ff_w1', 'ff_b1', 'ff_w2', 'ff_b2', 'd_q1', 'd_k1', 'd_v1', 'd_w1', 'd_q2', 'd_k2', 'd_v2', 'd_w2')}
    del _L3_xattn_all
    return {'x': x, 'ctx_1024': ctx_1024, 'L0_xattn_in_proj_w': _L0_xattn_in['in_proj_w'], 'L0_xattn_in_proj_b': _L0_xattn_in['in_proj_b'], 'L0_xattn_out_w': _L0_xattn_in['out_w'], 'L0_xattn_out_b': _L0_xattn_in['out_b'], 'L0_xattn_score_w': _L0_xattn_in['score_w'], 'L0_xattn_score_b': _L0_xattn_in['score_b'], 'L1_xattn_WQ1': _L1_xattn_in['WQ1'], 'L1_xattn_WK1': _L1_xattn_in['WK1'], 'L1_xattn_WV1': _L1_xattn_in['WV1'], 'L1_xattn_WQ2': _L1_xattn_in['WQ2'], 'L1_xattn_WK2': _L1_xattn_in['WK2'], 'L1_xattn_WV2': _L1_xattn_in['WV2'], 'L1_xattn_W_ff1': _L1_xattn_in['W_ff1'], 'L1_xattn_b_ff1': _L1_xattn_in['b_ff1'], 'L1_xattn_W_ff2': _L1_xattn_in['W_ff2'], 'L1_xattn_b_ff2': _L1_xattn_in['b_ff2'], 'L1_xattn_g1': _L1_xattn_in['g1'], 'L1_xattn_be1': _L1_xattn_in['be1'], 'L1_xattn_g2': _L1_xattn_in['g2'], 'L1_xattn_be2': _L1_xattn_in['be2'], 'L1_xattn_g3': _L1_xattn_in['g3'], 'L1_xattn_be3': _L1_xattn_in['be3'], 'L2_xattn_ln1_g': _L2_xattn_in['ln1_g'], 'L2_xattn_ln1_b': _L2_xattn_in['ln1_b'], 'L2_xattn_sa_wq': _L2_xattn_in['sa_wq'], 'L2_xattn_sa_bq': _L2_xattn_in['sa_bq'], 'L2_xattn_sa_wk': _L2_xattn_in['sa_wk'], 'L2_xattn_sa_bk': _L2_xattn_in['sa_bk'], 'L2_xattn_sa_wv': _L2_xattn_in['sa_wv'], 'L2_xattn_sa_bv': _L2_xattn_in['sa_bv'], 'L2_xattn_sa_wo': _L2_xattn_in['sa_wo'], 'L2_xattn_sa_bo': _L2_xattn_in['sa_bo'], 'L2_xattn_ln2_g': _L2_xattn_in['ln2_g'], 'L2_xattn_ln2_b': _L2_xattn_in['ln2_b'], 'L2_xattn_ca_wq': _L2_xattn_in['ca_wq'], 'L2_xattn_ca_bq': _L2_xattn_in['ca_bq'], 'L2_xattn_ca_wk': _L2_xattn_in['ca_wk'], 'L2_xattn_ca_bk': _L2_xattn_in['ca_bk'], 'L2_xattn_ca_wv': _L2_xattn_in['ca_wv'], 'L2_xattn_ca_bv': _L2_xattn_in['ca_bv'], 'L2_xattn_ca_wo': _L2_xattn_in['ca_wo'], 'L2_xattn_ca_bo': _L2_xattn_in['ca_bo'], 'L2_xattn_ln3_g': _L2_xattn_in['ln3_g'], 'L2_xattn_ln3_b': _L2_xattn_in['ln3_b'], 'L2_xattn_fc1_w': _L2_xattn_in['fc1_w'], 'L2_xattn_fc1_b': _L2_xattn_in['fc1_b'], 'L2_xattn_fc2_w': _L2_xattn_in['fc2_w'], 'L2_xattn_fc2_b': _L2_xattn_in['fc2_b'], 'L3_xattn_ln1_g': _L3_xattn_in['ln1_g'], 'L3_xattn_ln1_b': _L3_xattn_in['ln1_b'], 'L3_xattn_ln2_g': _L3_xattn_in['ln2_g'], 'L3_xattn_ln2_b': _L3_xattn_in['ln2_b'], 'L3_xattn_ln3_g': _L3_xattn_in['ln3_g'], 'L3_xattn_ln3_b': _L3_xattn_in['ln3_b'], 'L3_xattn_a1_wq': _L3_xattn_in['a1_wq'], 'L3_xattn_a1_wk': _L3_xattn_in['a1_wk'], 'L3_xattn_a1_wv': _L3_xattn_in['a1_wv'], 'L3_xattn_a1_wo': _L3_xattn_in['a1_wo'], 'L3_xattn_a1_bo': _L3_xattn_in['a1_bo'], 'L3_xattn_a2_wq': _L3_xattn_in['a2_wq'], 'L3_xattn_a2_wk': _L3_xattn_in['a2_wk'], 'L3_xattn_a2_wv': _L3_xattn_in['a2_wv'], 'L3_xattn_a2_wo': _L3_xattn_in['a2_wo'], 'L3_xattn_a2_bo': _L3_xattn_in['a2_bo'], 'L3_xattn_ff_w1': _L3_xattn_in['ff_w1'], 'L3_xattn_ff_b1': _L3_xattn_in['ff_b1'], 'L3_xattn_ff_w2': _L3_xattn_in['ff_w2'], 'L3_xattn_ff_b2': _L3_xattn_in['ff_b2'], 'L3_xattn_d_q1': _L3_xattn_in['d_q1'], 'L3_xattn_d_k1': _L3_xattn_in['d_k1'], 'L3_xattn_d_v1': _L3_xattn_in['d_v1'], 'L3_xattn_d_w1': _L3_xattn_in['d_w1'], 'L3_xattn_d_q2': _L3_xattn_in['d_q2'], 'L3_xattn_d_k2': _L3_xattn_in['d_k2'], 'L3_xattn_d_v2': _L3_xattn_in['d_v2'], 'L3_xattn_d_w2': _L3_xattn_in['d_w2']}

def reference(x, ctx_1024, L0_xattn_in_proj_w, L0_xattn_in_proj_b, L0_xattn_out_w, L0_xattn_out_b, L0_xattn_score_w, L0_xattn_score_b, L1_xattn_WQ1, L1_xattn_WK1, L1_xattn_WV1, L1_xattn_WQ2, L1_xattn_WK2, L1_xattn_WV2, L1_xattn_W_ff1, L1_xattn_b_ff1, L1_xattn_W_ff2, L1_xattn_b_ff2, L1_xattn_g1, L1_xattn_be1, L1_xattn_g2, L1_xattn_be2, L1_xattn_g3, L1_xattn_be3, L2_xattn_ln1_g, L2_xattn_ln1_b, L2_xattn_sa_wq, L2_xattn_sa_bq, L2_xattn_sa_wk, L2_xattn_sa_bk, L2_xattn_sa_wv, L2_xattn_sa_bv, L2_xattn_sa_wo, L2_xattn_sa_bo, L2_xattn_ln2_g, L2_xattn_ln2_b, L2_xattn_ca_wq, L2_xattn_ca_bq, L2_xattn_ca_wk, L2_xattn_ca_bk, L2_xattn_ca_wv, L2_xattn_ca_bv, L2_xattn_ca_wo, L2_xattn_ca_bo, L2_xattn_ln3_g, L2_xattn_ln3_b, L2_xattn_fc1_w, L2_xattn_fc1_b, L2_xattn_fc2_w, L2_xattn_fc2_b, L3_xattn_ln1_g, L3_xattn_ln1_b, L3_xattn_ln2_g, L3_xattn_ln2_b, L3_xattn_ln3_g, L3_xattn_ln3_b, L3_xattn_a1_wq, L3_xattn_a1_wk, L3_xattn_a1_wv, L3_xattn_a1_wo, L3_xattn_a1_bo, L3_xattn_a2_wq, L3_xattn_a2_wk, L3_xattn_a2_wv, L3_xattn_a2_wo, L3_xattn_a2_bo, L3_xattn_ff_w1, L3_xattn_ff_b1, L3_xattn_ff_w2, L3_xattn_ff_b2, L3_xattn_d_q1, L3_xattn_d_k1, L3_xattn_d_v1, L3_xattn_d_w1, L3_xattn_d_q2, L3_xattn_d_k2, L3_xattn_d_v2, L3_xattn_d_w2):
    import jax
    import jax.numpy as jnp

    def _L0_xattn_ref(base_hidden, scaffold_hidden, in_proj_w, in_proj_b, out_w, out_b, score_w, score_b):
        import jax, jax.numpy as jnp
        import numpy as np
        TOPK = 10
        NUM_HEADS = 16
        B, N, D = base_hidden.shape
        H = NUM_HEADS
        dh = D // H
        scores = jnp.einsum('bnd,d->bn', base_hidden, score_w[0]) + score_b[0]
        _, topk_idx = jax.lax.top_k(scores, TOPK)
        sparse_hidden = jnp.take_along_axis(base_hidden, topk_idx[:, :, None], axis=1)
        Wq, Wk, Wv = jnp.split(in_proj_w, 3, axis=0)
        bq, bk, bv = jnp.split(in_proj_b, 3)
        q = (sparse_hidden @ Wq.T + bq).reshape(B, TOPK, H, dh).transpose(0, 2, 1, 3)
        k = (scaffold_hidden @ Wk.T + bk).reshape(B, -1, H, dh).transpose(0, 2, 1, 3)
        v = (scaffold_hidden @ Wv.T + bv).reshape(B, -1, H, dh).transpose(0, 2, 1, 3)
        scale = 1.0 / np.sqrt(dh).astype(np.float32)
        logits = jnp.einsum('bhqd,bhkd->bhqk', q, k) * scale
        attn = jax.nn.softmax(logits, axis=-1)
        o = jnp.einsum('bhqk,bhkd->bhqd', attn, v).transpose(0, 2, 1, 3).reshape(B, TOPK, D)
        attn_out = o @ out_w.T + out_b
        return base_hidden.at[jnp.arange(B)[:, None], topk_idx].set(attn_out)

    def _L1_xattn_ref(y, Z, WQ1, WK1, WV1, WQ2, WK2, WV2, W_ff1, b_ff1, W_ff2, b_ff2, g1, be1, g2, be2, g3, be3):
        import jax, jax.numpy as jnp
        import numpy as np
        D_MODEL = 128
        D_FF = 512
        EPS = 1e-05

        def layer_norm(x, gamma, beta):
            mu = jnp.mean(x, axis=-1, keepdims=True)
            var = jnp.var(x, axis=-1, keepdims=True)
            return (x - mu) * jax.lax.rsqrt(var + EPS) * gamma + beta

        def attention(x_q, x_kv, WQ, WK, WV, causal):
            Q = x_q @ WQ
            K = x_kv @ WK
            V = x_kv @ WV
            scale = 1.0 / jnp.sqrt(jnp.asarray(Q.shape[-1], Q.dtype))
            scores = jnp.einsum('bqd,bkd->bqk', Q, K) * scale
            if causal:
                Sq, Sk = (scores.shape[-2], scores.shape[-1])
                mask = jnp.triu(jnp.full((Sq, Sk), -jnp.inf, scores.dtype), k=1)
                scores = scores + mask
            attn = jax.nn.softmax(scores, axis=-1)
            return jnp.einsum('bqk,bkd->bqd', attn, V)
        y = layer_norm(y + attention(y, y, WQ1, WK1, WV1, causal=True), g1, be1)
        y = layer_norm(y + attention(y, Z, WQ2, WK2, WV2, causal=False), g2, be2)
        h = jax.nn.relu(y @ W_ff1 + b_ff1) @ W_ff2 + b_ff2
        y = layer_norm(y + h, g3, be3)
        return y

    def _L2_xattn_ref(x, y, ln1_g, ln1_b, sa_wq, sa_bq, sa_wk, sa_bk, sa_wv, sa_bv, sa_wo, sa_bo, ln2_g, ln2_b, ca_wq, ca_bq, ca_wk, ca_bk, ca_wv, ca_bv, ca_wo, ca_bo, ln3_g, ln3_b, fc1_w, fc1_b, fc2_w, fc2_b):
        import jax, jax.numpy as jnp
        import numpy as np
        B, LX, LY = (2, 256, 256)
        E, H = (128, 16)
        HD = E // H
        FF = 512
        EPS = 1e-05

        def _rope_tables(L, d):
            inv = 1.0 / 10000.0 ** (jnp.arange(0, d, 2, dtype=jnp.float32) / d)
            t = jnp.arange(L, dtype=jnp.float32)
            f = jnp.outer(t, inv)
            return (jnp.cos(f), jnp.sin(f))

        def _apply_rope(x, cos, sin):
            d2 = x.shape[-1] // 2
            x1, x2 = (x[..., :d2], x[..., d2:])
            c = cos[None, :, None, :]
            s = sin[None, :, None, :]
            return jnp.concatenate([x1 * c - x2 * s, x2 * c + x1 * s], axis=-1)

        def _ln(x, g, b):
            m = jnp.mean(x, axis=-1, keepdims=True)
            v = jnp.var(x, axis=-1, keepdims=True)
            return (x - m) / jnp.sqrt(v + EPS) * g + b

        def _attn(q, k, v, causal):
            s = jnp.einsum('blhd,bmhd->bhlm', q, k)
            if causal:
                Lq, Lk = (s.shape[2], s.shape[3])
                mask = jnp.tril(jnp.ones((Lq, Lk), dtype=bool))
                s = jnp.where(mask, s, -jnp.inf)
            p = jax.nn.softmax(s, axis=-1)
            return jnp.einsum('bhlm,bmhd->blhd', p, v)

        def _forward(x, y, ln1_g, ln1_b, sa_wq, sa_bq, sa_wk, sa_bk, sa_wv, sa_bv, sa_wo, sa_bo, ln2_g, ln2_b, ca_wq, ca_bq, ca_wk, ca_bk, ca_wv, ca_bv, ca_wo, ca_bo, ln3_g, ln3_b, fc1_w, fc1_b, fc2_w, fc2_b):
            Bx, Lx, _ = x.shape
            Ly = y.shape[1]
            cos, sin = _rope_tables(max(Lx, Ly), HD)
            scale = HD ** (-0.5)
            h = _ln(x, ln1_g, ln1_b)
            q = (h @ sa_wq + sa_bq).reshape(Bx, Lx, H, HD) * scale
            k = (h @ sa_wk + sa_bk).reshape(Bx, Lx, H, HD)
            v = (h @ sa_wv + sa_bv).reshape(Bx, Lx, H, HD)
            q = _apply_rope(q, cos[:Lx], sin[:Lx])
            k = _apply_rope(k, cos[:Lx], sin[:Lx])
            a = _attn(q, k, v, causal=True).reshape(Bx, Lx, E)
            x = x + (a @ sa_wo + sa_bo)
            h = _ln(x, ln2_g, ln2_b)
            q = (h @ ca_wq + ca_bq).reshape(Bx, Lx, H, HD) * scale
            k = (y @ ca_wk + ca_bk).reshape(Bx, Ly, H, HD)
            v = (y @ ca_wv + ca_bv).reshape(Bx, Ly, H, HD)
            q = _apply_rope(q, cos[:Lx], sin[:Lx])
            k = _apply_rope(k, cos[:Ly], sin[:Ly])
            a = _attn(q, k, v, causal=False).reshape(Bx, Lx, E)
            x = x + (a @ ca_wo + ca_bo)
            h = _ln(x, ln3_g, ln3_b)
            return x + (jax.nn.gelu(h @ fc1_w + fc1_b) @ fc2_w + fc2_b)
        return _forward(x, y, ln1_g, ln1_b, sa_wq, sa_bq, sa_wk, sa_bk, sa_wv, sa_bv, sa_wo, sa_bo, ln2_g, ln2_b, ca_wq, ca_bq, ca_wk, ca_bk, ca_wv, ca_bv, ca_wo, ca_bo, ln3_g, ln3_b, fc1_w, fc1_b, fc2_w, fc2_b)

    def _L3_xattn_ref(x, context, ln1_g, ln1_b, ln2_g, ln2_b, ln3_g, ln3_b, a1_wq, a1_wk, a1_wv, a1_wo, a1_bo, a2_wq, a2_wk, a2_wv, a2_wo, a2_bo, ff_w1, ff_b1, ff_w2, ff_b2, d_q1, d_k1, d_v1, d_w1, d_q2, d_k2, d_v2, d_w2):
        import jax, jax.numpy as jnp
        import numpy as np
        B, N, M, D, H = (2, 256, 77, 128, 16)
        DH = D // H
        SCALE = DH ** (-0.5)
        EPS = 1e-05

        def _round_ste(x):
            return x + jax.lax.stop_gradient(jnp.round(x) - x)

        def _fq(x, delta, zp, n_bits):
            xi = _round_ste(x / delta) + zp
            xq = jnp.clip(xi, 0.0, 2.0 ** n_bits - 1.0)
            return (xq - zp) * delta

        def _ln(x, g, b):
            mu = jnp.mean(x, -1, keepdims=True)
            var = jnp.var(x, -1, keepdims=True)
            return (x - mu) * jax.lax.rsqrt(var + EPS) * g + b

        def _attn(x, ctx, wq, wk, wv, wo, bo, dq, dk, dv, dw):
            b, n, _ = x.shape
            m = ctx.shape[1]
            q = (x @ wq).reshape(b, n, H, DH).transpose(0, 2, 1, 3)
            k = (ctx @ wk).reshape(b, m, H, DH).transpose(0, 2, 1, 3)
            v = (ctx @ wv).reshape(b, m, H, DH).transpose(0, 2, 1, 3)
            sim = jnp.einsum('bhid,bhjd->bhij', _fq(q, dq, 128.0, 8), _fq(k, dk, 128.0, 8)) * SCALE
            attn = jax.nn.softmax(sim, axis=-1)
            out = jnp.einsum('bhij,bhjd->bhid', _fq(attn, dw, 0.0, 8), _fq(v, dv, 128.0, 8))
            out = out.transpose(0, 2, 1, 3).reshape(b, n, D)
            return out @ wo + bo
        h1 = _ln(x, ln1_g, ln1_b)
        x = _attn(h1, h1, a1_wq, a1_wk, a1_wv, a1_wo, a1_bo, d_q1, d_k1, d_v1, d_w1) + x
        h2 = _ln(x, ln2_g, ln2_b)
        x = _attn(h2, context, a2_wq, a2_wk, a2_wv, a2_wo, a2_bo, d_q2, d_k2, d_v2, d_w2) + x
        h3 = _ln(x, ln3_g, ln3_b)
        hg = h3 @ ff_w1 + ff_b1
        a, g = jnp.split(hg, 2, axis=-1)
        x = a * jax.nn.gelu(g, approximate=False) @ ff_w2 + ff_b2 + x
        return x
    x = _L0_xattn_ref(x, ctx_1024, L0_xattn_in_proj_w, L0_xattn_in_proj_b, L0_xattn_out_w, L0_xattn_out_b, L0_xattn_score_w, L0_xattn_score_b)
    x = _L1_xattn_ref(x, ctx_1024, L1_xattn_WQ1, L1_xattn_WK1, L1_xattn_WV1, L1_xattn_WQ2, L1_xattn_WK2, L1_xattn_WV2, L1_xattn_W_ff1, L1_xattn_b_ff1, L1_xattn_W_ff2, L1_xattn_b_ff2, L1_xattn_g1, L1_xattn_be1, L1_xattn_g2, L1_xattn_be2, L1_xattn_g3, L1_xattn_be3)
    x = _L2_xattn_ref(x, ctx_1024, L2_xattn_ln1_g, L2_xattn_ln1_b, L2_xattn_sa_wq, L2_xattn_sa_bq, L2_xattn_sa_wk, L2_xattn_sa_bk, L2_xattn_sa_wv, L2_xattn_sa_bv, L2_xattn_sa_wo, L2_xattn_sa_bo, L2_xattn_ln2_g, L2_xattn_ln2_b, L2_xattn_ca_wq, L2_xattn_ca_bq, L2_xattn_ca_wk, L2_xattn_ca_bk, L2_xattn_ca_wv, L2_xattn_ca_bv, L2_xattn_ca_wo, L2_xattn_ca_bo, L2_xattn_ln3_g, L2_xattn_ln3_b, L2_xattn_fc1_w, L2_xattn_fc1_b, L2_xattn_fc2_w, L2_xattn_fc2_b)
    x = _L3_xattn_ref(x, ctx_1024, L3_xattn_ln1_g, L3_xattn_ln1_b, L3_xattn_ln2_g, L3_xattn_ln2_b, L3_xattn_ln3_g, L3_xattn_ln3_b, L3_xattn_a1_wq, L3_xattn_a1_wk, L3_xattn_a1_wv, L3_xattn_a1_wo, L3_xattn_a1_bo, L3_xattn_a2_wq, L3_xattn_a2_wk, L3_xattn_a2_wv, L3_xattn_a2_wo, L3_xattn_a2_bo, L3_xattn_ff_w1, L3_xattn_ff_b1, L3_xattn_ff_w2, L3_xattn_ff_b2, L3_xattn_d_q1, L3_xattn_d_k1, L3_xattn_d_v1, L3_xattn_d_w1, L3_xattn_d_q2, L3_xattn_d_k2, L3_xattn_d_v2, L3_xattn_d_w2)
    return x

_drawn_inputs = setup_inputs


def setup_inputs(seed=0):
    import zlib

    import numpy as np

    out = dict(_drawn_inputs(seed))
    spreads = {'L1_xattn_b_ff1': (0.0, 0.291),
     'L1_xattn_b_ff2': (0.0, 0.1),
     'L1_xattn_g1': (1.0, 0.2),
     'L1_xattn_be1': (0.0, 0.1),
     'L1_xattn_g2': (1.0, 0.2),
     'L1_xattn_be2': (0.0, 0.1),
     'L1_xattn_g3': (1.0, 0.2),
     'L1_xattn_be3': (0.0, 0.1),
     'L2_xattn_ln1_g': (1.0, 0.6),
     'L2_xattn_ln1_b': (0.0, 0.8),
     'L2_xattn_sa_bq': (0.0, 0.8),
     'L2_xattn_sa_bk': (0.0, 0.8),
     'L2_xattn_sa_bv': (0.0, 0.366),
     'L2_xattn_sa_bo': (0.0, 0.1),
     'L2_xattn_ln2_g': (1.0, 0.6),
     'L2_xattn_ln2_b': (0.0, 0.8),
     'L2_xattn_ca_bq': (0.0, 2.0),
     'L2_xattn_ca_bk': (0.0, 2.0),
     'L2_xattn_ca_bv': (0.0, 0.388),
     'L2_xattn_ca_bo': (0.0, 0.1),
     'L2_xattn_ln3_g': (1.0, 0.6),
     'L2_xattn_ln3_b': (0.0, 0.8),
     'L2_xattn_fc1_b': (0.0, 0.298),
     'L2_xattn_fc2_b': (0.0, 0.1),
     'L3_xattn_ln1_g': (1.0, 0.6),
     'L3_xattn_ln1_b': (0.0, 0.8),
     'L3_xattn_ln2_g': (1.0, 0.6),
     'L3_xattn_ln2_b': (0.0, 0.8),
     'L3_xattn_ln3_g': (1.0, 0.6),
     'L3_xattn_ln3_b': (0.0, 0.8),
     'L3_xattn_a1_bo': (0.0, 0.1),
     'L3_xattn_a2_bo': (0.0, 0.1),
     'L3_xattn_ff_b1': (0.0, 0.8),
     'L3_xattn_ff_b2': (0.0, 0.1)}
    factors = {'L0_xattn_in_proj_b': 8.0,
     'L0_xattn_out_b': 8.0,
     'L1_xattn_WQ1': 8.0,
     'L1_xattn_WK1': 8.0,
     'L1_xattn_WQ2': 8.0,
     'L1_xattn_WK2': 8.0,
     'L2_xattn_sa_wq': 8.0,
     'L2_xattn_sa_wk': 8.0,
     'L2_xattn_sa_wv': 4.144,
     'L2_xattn_ca_wq': 8.0,
     'L2_xattn_ca_wk': 8.0,
     'L3_xattn_a1_wq': 8.0,
     'L3_xattn_a1_wk': 8.0,
     'L3_xattn_a1_wv': 4.018,
     'L3_xattn_a1_wo': 4.49,
     'L3_xattn_a2_wq': 8.0,
     'L3_xattn_a2_wk': 8.0,
     'L3_xattn_a2_wo': 2.69,
     'L3_xattn_ff_w1': 3.826,
     'L3_xattn_ff_w2': 3.771}
    for name, (base, spread) in spreads.items():
        noise = np.random.default_rng([zlib.crc32(name.encode()), seed]).standard_normal(out[name].shape)
        drawn = base * np.exp(spread * noise) if base else spread * noise
        out[name] = jnp.asarray(drawn.astype(out[name].dtype))
    for name, factor in factors.items():
        out[name] = (out[name] * factor).astype(out[name].dtype)
    return out
```

```python
from contextlib import ExitStack

import numpy as np
import concourse.bass as bass
from concourse import mybir

F32 = mybir.dt.float32
BF16 = mybir.dt.bfloat16
ALU = mybir.AluOpType
ACT = mybir.ActivationFunctionType
AX = mybir.AxisListType.X

P = 128
D = 128
B, N, M = 2, 512, 77
H = 16
DH = D // H
QB = N // P
T = B * QB
NT = B * N
U = B * H
TOPK = 10
FF = 512
FC = FF // P
EPS = 1e-5
MASKED = -1e30
MAGIC = 1.5 * 2.0 ** 23
TAKEN = -3.0e38
QMAX = 255.0
ZERO_POINT = 128.0
HEAD_SCALE = float(np.float32(DH ** -0.5))
ONE_SCALE = float(np.float32(1.0) / np.sqrt(np.float32(D)))

COLUMNS = [("L0_xattn_in_proj_b", 2), ("L0_xattn_score_w", 1), ("L1_xattn_b_ff1", 4),
           ("L2_xattn_ln1_g", 1), ("L2_xattn_ln1_b", 1), ("L2_xattn_sa_bq", 1), ("L2_xattn_sa_bk", 1),
           ("L2_xattn_ln2_g", 1), ("L2_xattn_ln2_b", 1), ("L2_xattn_ca_bq", 1), ("L2_xattn_ca_bk", 1),
           ("L2_xattn_ln3_g", 1), ("L2_xattn_ln3_b", 1), ("L2_xattn_fc1_b", 4),
           ("L3_xattn_ln1_g", 1), ("L3_xattn_ln1_b", 1), ("L3_xattn_ln2_g", 1), ("L3_xattn_ln2_b", 1),
           ("L3_xattn_ln3_g", 1), ("L3_xattn_ln3_b", 1), ("L3_xattn_ff_b1", 8)]
NCOL = sum(n for _, n in COLUMNS)
COL = {}
for _name, _n in COLUMNS:
    COL[_name] = sum(m for k, m in COLUMNS[:len(COL)])
ROWS = ["L0_bv", "L0_xattn_out_b", "L1_xattn_b_ff2", "L2_xattn_sa_bv", "L2_xattn_sa_bo", "L2_xattn_ca_bv",
        "L2_xattn_ca_bo", "L2_xattn_fc2_b", "L3_xattn_a1_bo", "L3_xattn_a2_bo", "L3_xattn_ff_b2"]
SPREAD = ["L1_xattn_g1", "L1_xattn_be1", "L1_xattn_g2", "L1_xattn_be2", "L1_xattn_g3", "L1_xattn_be3"]
SCALARS = ["L3_xattn_d_q1", "L3_xattn_d_k1", "L3_xattn_d_v1", "L3_xattn_d_w1",
           "L3_xattn_d_q2", "L3_xattn_d_k2", "L3_xattn_d_v2", "L3_xattn_d_w2", "L0_xattn_score_b"]
DQ1, DK1, DV1, DW1, DQ2, DK2, DV2, DW2, SCORE_B = range(9)
SQUARE = ["L1_xattn_WK2", "L1_xattn_WV2", "L2_xattn_ca_wk", "L2_xattn_ca_wv", "L3_xattn_a2_wk", "L3_xattn_a2_wv",
          "L1_xattn_WQ1", "L1_xattn_WK1", "L1_xattn_WV1", "L1_xattn_WQ2",
          "L2_xattn_sa_wq", "L2_xattn_sa_wk", "L2_xattn_sa_wv", "L2_xattn_sa_wo",
          "L2_xattn_ca_wq", "L2_xattn_ca_wo",
          "L3_xattn_a1_wq", "L3_xattn_a1_wk", "L3_xattn_a1_wv", "L3_xattn_a1_wo",
          "L3_xattn_a2_wq", "L3_xattn_a2_wo"]

SQUARE_LOAD = 6

TERMS = [(0, 0), (0, 1), (1, 0), (1, 1), (0, 2), (2, 0), (1, 2), (2, 1)]
SHIFT_ROW = len(TERMS) * DH
STACK = SHIFT_ROW + 2
KEY_TILE_AT = {0: 0, 1: 512, 3: 896, 2: 1024}
CAUSAL_COLS = 1280
HIDDEN = (2, 3, 6, 7)
CROSS_GROUPS = [(0, 6), (6, 6), (12, 4)]


STOP = 3


def rope_tables():
    inv = np.float32(1.0) / np.float32(10000.0) ** (np.arange(0, DH, 2, dtype=np.float32) / np.float32(DH))
    f = np.outer(np.arange(N, dtype=np.float32), inv.astype(np.float32)).astype(np.float32)
    c, s = np.cos(f).astype(np.float32).T, np.sin(f).astype(np.float32).T
    return np.stack([np.tile(np.concatenate([c, c]), (H, 1)), np.tile(np.concatenate([-s, s]), (H, 1))])


def build(nc, ins, out, stop=99):
    ctx = ExitStack()
    with ctx:
        def sb(name, shape, dt=F32):
            return ctx.enter_context(nc.sbuf_tensor(name, shape, dt))

        sems = {}

        families = {
            "one": (["L1.sa", "L1.ca"], dict(s=T, exp=T, t=T, pt=T, o=T, m=T, x=T)),
            "cross": (["L2.ca", "L3.ca"], dict(s=T, sub=T, p=T, t=4 * T, pt=4 * T, o=4 * T, rows=T, q=B)),
            "ff": (["L1.ff", "L2.ff", "L3.ff"], dict(h=B * FC, hid=B * FC)),
            "add": (["L1.ff", "L2.ca0", "L2.co", "L2.ff", "L3.ca0", "L3.co", "L3.ff"], dict(o=B, x=B)),
            "postnorm": (["L1.ln1", "L1.ln2", "L1.ln3"], dict(scaled=B, x=B)),
            "norm": (["L2.ln1", "L2.ln2", "L2.ln3", "L3.ln1", "L3.ln2", "L3.ln3"], dict(xh=B)),
        }
        shared = {}
        for family, (stages, signals) in families.items():
            for signal, n in signals.items():
                for i, stage in enumerate(stages):
                    shared[f"{stage}.{signal}"] = (f"{family}.{signal}", i * n)

        def count(stage, signal):
            return shared.get(f"{stage}.{signal}", ("", 0))[1]

        def S(name):
            name = shared.get(name, (name, 0))[0]
            if name not in sems:
                sems[name] = ctx.enter_context(nc.semaphore(name.replace(".", "_")))
            return sems[name]

        rope_dram = nc.inline_tensor(rope_tables(), name="rope_tables").ap()
        parts_dram = nc.dram_tensor("parts_dram", (2, 3, D, NT), BF16, kind="Internal").ap()

        x = sb("x", [P, T, D])
        ctx_rows = sb("ctx_rows", [M, B, D])
        col_rows = sb("col_rows", [NCOL, P])
        cols = sb("cols", [P, NCOL])
        rows = sb("rows", [1, len(ROWS), D])
        spread = sb("spread", [P, len(SPREAD), D])
        scalar_row = sb("scalar_row", [1, 9])
        scalars = sb("scalars", [P, 9])
        in_proj = sb("in_proj", [P, 4, D])
        wT = sb("wT", [P, 4, D])
        wsq = sb("wsq", [P, len(SQUARE), D])
        W = {n: wsq[:, i, :] for i, n in enumerate(SQUARE)}
        l1_w1, l1_w2 = sb("l1_w1", [P, FF]), sb("l1_w2", [P, FC, D])
        l2_w1, l2_w2 = sb("l2_w1", [P, FF]), sb("l2_w2", [P, FC, D])
        l3_w1, l3_w2 = sb("l3_w1", [P, 2 * FF]), sb("l3_w2", [P, FC, D])
        cos_t, sin_t = sb("cos_t", [P, N]), sb("sin_t", [P, N])

        ident, ident16 = sb("ident", [P, P]), sb("ident16", [P, P], BF16)
        swap = sb("swap", [P, P])
        hide_q = sb("hide_q", [P, P], BF16)
        hide_k = sb("hide_k", [P, P], BF16)
        head_mask = sb("head_mask", [P, H])
        ones_row = sb("ones_row", [1, P])
        ranks = sb("ranks", [P, TOPK])
        minus_half = sb("minus_half", [P, QB])
        c255 = sb("c255", [P, P], BF16)
        relu_top = sb("relu_top", [P, 1])
        tick = sb("tick", [P, 1])
        magic_col = sb("magic_col", [P, 1])

        e_buf = sb("e_buf", [P, 2, 2048])
        t_buf = sb("t_buf", [P, 2, 2048], BF16)
        pt_buf = sb("pt_buf", [P, 2, 512])
        xT = sb("xT", [P, NT])
        xh = sb("xh", [P, T, D])
        ctxT = sb("ctxT", [P, B * M])
        qT, kT = sb("qT", [P, NT]), sb("kT", [P, NT])
        ta, tb = sb("ta", [P, NT]), sb("tb", [P, NT])
        v_rows = sb("v_rows", [P, T, D])
        hid = e_buf[:, :, :].rearrange("p a (c n) -> p (a c) n", n=NT)
        gel = sb("gel", [P, 2, N])
        st = sb("st", [P, T, 6])
        mv = sb("mv", [P, T, 2])
        rstd = sb("rstd", [P, T])
        kc = sb("kc", [P, 4, B * M])
        vc = sb("vc", [M, 4, B, D])
        vc3 = sb("vc3", [M, B, D], BF16)
        km2 = sb("km2", [P, B, H, M])
        km3 = sb("km3", [P, B, H, M], BF16)
        stats = sb("stats", [P, 8, 16])
        q_stack = sb("q_stack", [P, U * N], BF16)
        k_stack = sb("k_stack", [P, U * N], BF16)
        v_neg = q_stack[:, 3 * NT:4 * NT].rearrange("p (t d) -> p t d", d=D)
        cv = sb("cv", [P, B, D])
        sders = sb("sders", [P, 16])
        row_recip = sb("row_recip", [P, QB, H])
        cr_max, cr_sum, cr_rec = (sb(n, [P, 2, H]) for n in ("cr_max", "cr_sum", "cr_rec"))
        z3 = sb("z3", [P, 3])
        l0_sc, l0_left, l0_zero, tokrank = (e_buf[0:B, 0, k * N:(k + 1) * N] for k in range(4))
        l0_best = sb("l0_best", [B, 8])
        l0_next = sb("l0_next", [B, 8])
        onehot = sb("onehot", [P, B, QB, TOPK])
        onehotT = gel[0:TOPK, :, :].rearrange("r b (t n) -> r b t n", n=P)
        kept = sb("kept", [P, T])
        l0_xs = sb("l0_xs", [P, B * TOPK])
        l0_q = sb("l0_q", [P, B * TOPK])
        l0_qblk = e_buf[:, 1, 0:B * H * TOPK].rearrange("p (b n) -> p b n", b=B)
        l0_p = e_buf[0:80, 1, 512:512 + 4 * M].rearrange("p (n m) -> p n m", m=M)
        l0_st = sb("l0_st", [80, 3, 4])
        l0_pt = e_buf[0:M, 1, 1024:1024 + B * H * TOPK]
        l0_od = e_buf[:, 1, 1536:1536 + B * H * TOPK].rearrange("p (b h q) -> p b h q", b=B, h=H)
        l0_ot = sb("l0_ot", [P, B, TOPK])
        l0_ao = sb("l0_ao", [TOPK, B, D])
        parts = e_buf[:, :, :].rearrange("p a n -> p (a n)")[:, 0:3 * NT].bitcast(BF16).rearrange(
            "p (s k n) -> p s k n", s=2, k=3)
        q_int, k_int = q_stack[:, 0:NT], q_stack[:, NT:2 * NT]
        v_int = q_stack[:, 2 * NT:3 * NT].rearrange("p (t d) -> p t d", d=D)
        v_one = sb("v_one", [P, QB, U, DH + 1])
        neg_max = sb("neg_max", [P, U * QB])
        shift = sb("shift", [P, 2, P], BF16)

        ps = ctx.enter_context(nc.psum_tensor("ps", [P, 8, 512], F32))
        ps_flat = ps[:, :, :].rearrange("p b c -> p (b c)")

        def tile(a, i):
            return a[:, i * P:(i + 1) * P]

        def col(name, k=0):
            return cols[:, COL[name] + k:COL[name] + k + 1]

        def row(name):
            return rows[0:1, ROWS.index(name), :]

        def sc(k):
            return scalars[:, k:k + 1]

        def half(a, i):
            return a[:, i * N:(i + 1) * N]

        def half_rows(a, i):
            return a[:, i * QB:(i + 1) * QB, :]

        def bank_rows(k):
            return ps[:, k, :].rearrange("p (t d) -> p t d", d=D)

        x_dram = ins["x"].rearrange("b (t p) d -> p (b t) d", p=P)
        out_dram = out.rearrange("b (t p) d -> p (b t) d", p=P)

        ln_index = {}
        for layer in ("L1", "L2", "L3"):
            for k in range(3):
                ln_index[f"{layer}.ln{k + 1}"] = len(ln_index)

        turns = ["L1.sa", "L1.ca", "L1.ff", "L2.sa", "L2.ca0", "L2.ca", "L2.co", "L2.ff",
                 "L3.sa", "L3.ca0", "L3.ca", "L3.co", "L3.ff"]

        def state(name, k):
            return B * turns.index(name) + k + 1

        final, final_each = {0: ("L0.x", QB), 1: ("L1.ln3.x", 1), 2: ("L2.ff.x", 1)}.get(stop, ("L3.ff.x", 1))
        block = ctx.enter_context(nc.Block())

        @block.sync
        def _(sp):
            sp.dma_start(x[:, :, :], x_dram).then_inc(S("x.loaded"), 16)
            sp.dma_start(in_proj[:, 0:3, :], ins["L0_xattn_in_proj_w"].rearrange("(t p) d -> p t d", p=P)
                         ).then_inc(S("inproj.loaded"), 16)
            sp.dma_start(in_proj[:, 3, :], ins["L0_xattn_out_w"]).then_inc(S("inproj.loaded"), 16)
            sp.dma_start(ctx_rows[:, :, :], ins["ctx_1024"].rearrange("b m d -> m b d")).then_inc(S("ctx.loaded"), 16)
            sp.dma_start(col_rows[:, :], ins["columns"]).then_inc(S("cols.loaded"), 16)
            sp.dma_start(scalar_row[:, :], ins["scalars"]).then_inc(S("scalars.loaded"), 16)
            sp.dma_start(rows[:, :, :], ins["rows"]).then_inc(S("rows.loaded"), 16)
            for k in range(0, len(SQUARE), SQUARE_LOAD):
                n = min(SQUARE_LOAD, len(SQUARE) - k)
                sp.dma_start(wsq[:, k:k + n, :], ins["squares"][k:k + n].rearrange("n p d -> p n d")
                             ).then_inc(S("weights.loaded" if k else "ctxw.loaded"), 16)
            sp.dma_start(cos_t[:, :], rope_dram[0]).then_inc(S("rope.loaded"), 16)
            sp.dma_start(sin_t[:, :], rope_dram[1]).then_inc(S("rope.loaded"), 16)
            sp.dma_start(spread[:, :, :].rearrange("p n d -> p (n d)"), ins["spread"].broadcast_to([P, len(SPREAD) * D])
                         ).then_inc(S("spread.loaded"), 16)
            for w1, w2, n1, n2 in ((l1_w1, l1_w2, "L1_xattn_W_ff1", "L1_xattn_W_ff2"),
                                   (l2_w1, l2_w2, "L2_xattn_fc1_w", "L2_xattn_fc2_w"),
                                   (l3_w1, l3_w2, "L3_xattn_ff_w1", "L3_xattn_ff_w2")):
                sp.dma_start(w1[:, :], ins[n1]).then_inc(S("ffw.loaded"), 16)
                sp.dma_start(w2[:, :, :], ins[n2].rearrange("(c p) d -> p c d", p=P)).then_inc(S("ffw.loaded"), 16)
            if stop >= 2:
                for side, (name, stack) in enumerate((("q", q_stack), ("k", k_stack))):
                    for part in range(3):
                        sp.wait_ge(S(f"L2.{name}.parts"), part + 1)
                        sp.dma_start(parts_dram[side, part], parts[:, side, part, :]).then_inc(S(f"L2.{name}.stored"), 16)
                    sp.wait_ge(S(f"L2.{name}.stored"), 48)
                    for s, term in enumerate(TERMS):
                        for b in range(B):
                            dst = stack[s * DH:(s + 1) * DH, b * H * N:(b + 1) * H * N]
                            src = parts_dram[side, term[side], :, b * N:(b + 1) * N]
                            sp.dma_start(dst.rearrange("d (h n) -> d h n", h=H),
                                         src.rearrange("(h d) n -> d h n", d=DH)).then_inc(S("L2.stacked"), 16)
                sp.wait_ge(S("L2.shift"), 2)
                for r in range(2):
                    sp.dma_start(q_stack[SHIFT_ROW + r:SHIFT_ROW + r + 1, :].rearrange("o (r c) -> o r c", c=P),
                                 shift[:, r, :]).then_inc(S("L2.shift.placed"), 16)
            for k in range(B):
                sp.wait_ge(S(final), count(*final.rsplit(".", 1)) + final_each * (k + 1))
                sp.dma_start(half_rows(out_dram, k), half_rows(x, k)).then_inc(S("out.stored"), 16)
            sp.wait_ge(S("out.stored"), 16 * B)

        @block.gpsimd
        def _(pool):
            def select(m, pattern, base, mult, fill, op, src=None):
                return pool.affine_select(out=m, in_=m if src is None else src, compare_op=op, fill=fill, base=base,
                                          pattern=pattern, channel_multiplier=mult)

            pool.memset(ident[:, :], 0.0).then_inc(S("const.base"), 1)
            pool.memset(ident16[:, :], 0.0).then_inc(S("const.base"), 1)
            pool.memset(hide_q[:, :], 0.0).then_inc(S("const.base"), 1)
            pool.memset(hide_k[:, :], 0.0).then_inc(S("const.base"), 1)
            pool.memset(head_mask[:, :], 1.0).then_inc(S("const.base"), 1)
            pool.memset(ones_row[:, :], 1.0).then_inc(S("const.base"), 1)
            pool.memset(minus_half[:, :], -0.5).then_inc(S("const.base"), 1)
            pool.memset(c255[:, :], QMAX).then_inc(S("const.base"), 1)
            pool.memset(relu_top[:, :], MAGIC + QMAX).then_inc(S("const.base"), 1)
            for r in range(TOPK):
                pool.memset(ranks[:, r:r + 1], float(r + 1)).then_inc(S("const.base"), 1)
            pool.wait_ge(S("const.base"), 9 + TOPK)
            select(ident[:, :], [[-1, P]], 0, 1, 1.0, ALU.not_equal).then_inc(S("const.made"), 1)
            select(ident16[:, :], [[-1, P]], 0, 1, 1.0, ALU.not_equal).then_inc(S("const.made"), 1)
            select(hide_q[:, :], [[-1, P]], 0, 1, MASKED, ALU.is_ge).then_inc(S("const.made"), 1)
            select(hide_k[:, :], [[1, P]], 0, -1, MASKED, ALU.is_ge).then_inc(S("const.made"), 1)
            select(head_mask[:, :], [[-DH, H]], 0, 1, 0.0, ALU.is_ge).then_inc(S("const.made"), 1)
            pool.wait_ge(S("const.made"), 5)
            select(head_mask[:, :], [[DH, H]], DH - 1, -1, 0.0, ALU.is_ge).then_inc(S("const.made"), 1)
            sw, idn = (a[:, :].rearrange("p (h s d) -> p h s d", s=2, d=DH // 2) for a in (swap, ident))
            pool.tensor_copy(sw[:, :, 0, :], idn[:, :, 1, :]).then_inc(S("const.made"), 1)
            pool.tensor_copy(sw[:, :, 1, :], idn[:, :, 0, :]).then_inc(S("const.made"), 1)
            pool.memset(v_one[:, :, :, DH:DH + 1], 1.0).then_inc(S("stack.ones"), 1)
            pool.wait_ge(S("stack.ones"), 1)
            pool.memset(q_stack[SHIFT_ROW:STACK, :].bitcast(F32), 0.0).then_inc(S("stack.ones"), 1)
            pool.wait_ge(S("stack.ones"), 2)
            pool.memset(k_stack[SHIFT_ROW:STACK, :], 1.0).then_inc(S("stack.ones"), 1)

            def masked_keys(dst, src, b):
                pool.tensor_tensor(dst[:, b, :, :], src[:, b * M:(b + 1) * M].unsqueeze(1).broadcast_to([P, H, M]),
                                   head_mask[:, :].unsqueeze(2).broadcast_to([P, H, M]), ALU.mult
                                   ).then_inc(S("ctx.masked"), 1)

            pool.wait_ge(S("stack.ones"), 3)
            pool.wait_ge(S("const.made"), 8)
            pool.wait_ge(S("ctx.rope"), 1)
            for b in range(B):
                masked_keys(km2, kc[:, 2, :], b)
            pool.wait_ge(S("ctx.quant"), 2)
            for b in range(B):
                masked_keys(km3, kc[:, 3, :], b)

            def rstds(name):
                for k in range(B):
                    r = rstd[:, k * QB:(k + 1) * QB]
                    pool.wait_ge(S("ln.mv"), B * ln_index[name] + k + 1)
                    pool.tensor_scalar(r, mv[:, k * QB:(k + 1) * QB, 1], EPS, None, ALU.add).then_inc(S("ln.ve"), 1)
                    pool.wait_ge(S("ln.ve"), B * ln_index[name] + k + 1)
                    pool.tensor_tensor(r, r, minus_half[:, :], ALU.pow).then_inc(S("ln.rstd"), 1)

            def post_norm(name, g, be):
                for k in range(B):
                    pool.wait_ge(S(f"{name}.scaled"), count(name, "scaled") + k + 1)
                    pool.tensor_tensor(half_rows(x, k), half_rows(xh, k),
                                       spread[:, be, :].unsqueeze(1).broadcast_to([P, QB, D]), ALU.add
                                       ).then_inc(S(f"{name}.x"), 1)

            pool.wait_ge(S("spread.loaded"), 16)
            for k in range(3):
                if stop >= 1:
                    rstds(f"L1.ln{k + 1}")
                    post_norm(f"L1.ln{k + 1}", 2 * k, 2 * k + 1)
            for layer in ("L2", "L3"):
                for k in range(3):
                    if stop >= int(layer[1]):
                        rstds(f"{layer}.ln{k + 1}")
                    if layer == "L3" and k == 0 and stop >= 3:
                        def round_unit(u, p):
                            pool.wait_ge(S("L3.recip"), u + 1)
                            pool.tensor_tensor(tick[:, :], minus_half[:, 0:1], minus_half[:, 0:1], ALU.mult
                                               ).then_inc(S("L3.tick"), 1)
                            for qb in range(QB):
                                e = e_buf[:, p, qb * N:(qb + 1) * N]
                                pool.tensor_scalar(e, e, stats[:, 4 + p, qb:qb + 1], MAGIC, ALU.mult, ALU.add
                                                   ).then_inc(S("L3.rounded"), 1)
                        with pool.Fori(0, U // 2) as i:
                            for p in range(2):
                                round_unit(2 * i + p, p)

        @block.tensor
        def _(pe):
            def turn_state(name, src, ready, each=1):
                for k in range(B):
                    pe.wait_ge(S(ready), count(*ready.rsplit(".", 1)) + each * (k + 1))
                    for t in range(QB):
                        mm = pe.transpose(ps[:, k, t * P:(t + 1) * P], src[:, k * QB + t, :], ident[:, :])
                    mm.then_inc(S("state.turned"), 1)

            def project(name, w, k, bank):
                return pe.matmul(ps[:, bank, :], w, half(xT, k), start=True, stop=True)

            def qkv(name, wq, wk, wv, bv=None):
                for k in range(B):
                    pe.wait_ge(S("state.T"), state(name, k))
                    project(name, wq, k, 2 + k).then_inc(S(f"{name}.q.mm"), 1)
                    project(name, wk, k, 4 + k).then_inc(S(f"{name}.k.mm"), 1)
                    for t in range(QB):
                        o = ps[:, 6 + k, t * P:(t + 1) * P]
                        mm = pe.matmul(o, tile(xT, k * QB + t), wv, start=True, stop=bv is None)
                        if bv is not None:
                            mm = pe.matmul(o, ones_row[:, :], row(bv), start=False, stop=True)
                    mm.then_inc(S(f"{name}.v.mm"), 1)

            def single_attention(name, q_ready, q_count, keys, width, values, causal):
                def scores(i):
                    if i >= 2:
                        pe.wait_ge(S("one.exp"), count(name, "exp") + i - 1)
                    n = width(i)
                    mm = pe.matmul(ps[:, 2 + i % 2, 0:n], tile(qT, i), keys(i), start=True, stop=not causal)
                    if causal:
                        mm = pe.matmul(ps[:, 2 + i % 2, n - P:n], ident16[:, :], hide_q[:, :], start=False, stop=True)
                    mm.then_inc(S("one.s"), 1)

                def turn(i):
                    pe.wait_ge(S("one.exp"), count(name, "exp") + i + 1)
                    if i >= 2:
                        pe.wait_ge(S("one.pt"), count(name, "pt") + i - 1)
                    n = width(i)
                    for c in range(0, n, P):
                        w = min(P, n - c)
                        mm = pe.transpose(ps[0:w, 4 + i % 2, c:c + P], e_buf[:, i % 2, c:c + w], ident[:, :])
                    mm.then_inc(S("one.t"), 1)

                def outputs(i):
                    pe.wait_ge(S("one.pt"), count(name, "pt") + i + 1)
                    if i >= 2:
                        pe.wait_ge(S("one.x"), count(name, "x") + i - 1)
                    n = width(i)
                    for c in range(0, n, P):
                        w = min(P, n - c)
                        mm = pe.matmul(ps[:, 6 + i % 2, 0:P], pt_buf[0:w, i % 2, c:c + P], values(i, c // P),
                                       start=(c == 0), stop=(c + P >= n))
                    mm.then_inc(S("one.o"), 1)

                pe.wait_ge(S(q_ready), q_count)
                for i in range(T + 2):
                    if i < T:
                        scores(i)
                    if 1 <= i <= T:
                        turn(i - 1)
                    if i >= 2:
                        outputs(i - 2)

            def feed_forward(name, w1, w2, b2, gated=False):
                pe.wait_ge(S("ffw.loaded"), 96)
                for k in range(B):
                    pe.wait_ge(S("state.T"), state(name, k))
                    for c in range(FC):
                        n = k * FC + c
                        if gated:
                            if n >= 2:
                                pe.wait_ge(S("ff.hid"), count(name, "hid") + n - 1)
                            pe.matmul(ps[:, HIDDEN[2 * (n % 2)], :], tile(w1, c), half(xT, k), start=True, stop=True)
                            mm = pe.matmul(ps[:, HIDDEN[2 * (n % 2) + 1], :], tile(w1, FC + c), half(xT, k),
                                           start=True, stop=True)
                        else:
                            if n >= 4:
                                pe.wait_ge(S("ff.hid"), count(name, "hid") + n - 3)
                            mm = pe.matmul(ps[:, HIDDEN[n % 4], :], tile(w1, c), half(xT, k), start=True, stop=True)
                        mm.then_inc(S("ff.h"), 1)
                for k in range(B):
                    pe.wait_ge(S("ff.hid"), count(name, "hid") + FC * (k + 1))
                    for t in range(QB):
                        o = ps[:, 4 + k, t * P:(t + 1) * P]
                        for c in range(FC):
                            pe.matmul(o, tile(hid[:, c, :], k * QB + t), w2[:, c, :], start=(c == 0), stop=False)
                        mm = pe.matmul(o, ones_row[:, :], row(b2), start=False, stop=True)
                    mm.then_inc(S("add.o"), 1)

            def out_project(name, wo, bo, rows_ready, each=1):
                turn_state(name, xh, rows_ready, each)
                for k in range(B):
                    pe.wait_ge(S("state.T"), state(name, k))
                    for t in range(QB):
                        o = ps[:, 2 + k, t * P:(t + 1) * P]
                        pe.matmul(o, tile(xT, k * QB + t), wo, start=True, stop=False)
                        mm = pe.matmul(o, ones_row[:, :], row(bo), start=False, stop=True)
                    mm.then_inc(S(f"{name}.o"), 1)

            def cross(name, keys, values, v_dtype):
                def scores(i):
                    if i >= 1:
                        pe.wait_ge(S("cross.sub"), count(name, "sub") + i)
                    q = tile(q_int if v_dtype == BF16 else qT, i)
                    for g, (h0, n) in enumerate(CROSS_GROUPS):
                        mm = pe.matmul(ps[:, g, 0:n * M], q, keys[:, i // QB, h0:h0 + n, :], start=True, stop=True)
                    mm.then_inc(S("cross.s"), 1)

                def turn(i, c):
                    n = 4 * i + c
                    pe.wait_ge(S("cross.p"), count(name, "p") + i + 1)
                    if n >= 2:
                        pe.wait_ge(S("cross.pt"), count(name, "pt") + n - 1)
                    for j in range(4):
                        h = 4 * c + j
                        mm = pe.transpose(ps[0:M, 3 + c % 2, j * P:(j + 1) * P],
                                          e_buf[:, i % 2, h * M:(h + 1) * M], ident[:, :])
                    mm.then_inc(S("cross.t"), 1)

                def outputs(i, c):
                    n = 4 * i + c
                    pe.wait_ge(S("cross.pt"), count(name, "pt") + n + 1)
                    if c == 0 and i >= 2:
                        pe.wait_ge(S("cross.rows"), count(name, "rows") + i - 1)
                    src = t_buf if v_dtype == BF16 else pt_buf
                    for j in range(4):
                        h = 4 * c + j
                        mm = pe.matmul(ps[:, 6 + i % 2, h * DH:(h + 1) * DH], src[0:M, c % 2, j * P:(j + 1) * P],
                                       values(i // QB)[:, h * DH:(h + 1) * DH], start=True, stop=True)
                    mm.then_inc(S("cross.o"), 1)

                pe.wait_ge(S("cross.q"), count(name, "q") + B)
                for i in range(T + 1):
                    if i < T:
                        scores(i)
                    if i >= 1:
                        for c in range(5):
                            if c < 4:
                                turn(i - 1, c)
                            if c >= 1:
                                outputs(i - 1, c - 1)

            pe.wait_ge(S("const.made"), 8)
            pe.wait_ge(S("x.loaded"), 16)
            for k in range(B):
                for t in range(QB):
                    mm = pe.transpose(ps[:, k, t * P:(t + 1) * P], x[:, k * QB + t, :], ident[:, :])
                mm.then_inc(S("L0.turned"), 1)
            pe.wait_ge(S("cols.loaded"), 16)
            pe.transpose(ps[:, 2, 0:NCOL], col_rows[:, :], ident[0:NCOL, 0:NCOL]).then_inc(S("cols.turned"), 1)
            pe.wait_ge(S("scalars.loaded"), 16)
            pe.matmul(ps[:, 2, 64:73], ones_row[:, :], scalar_row[:, :], start=True, stop=True
                      ).then_inc(S("cols.turned"), 1)
            pe.wait_ge(S("ctx.loaded"), 16)
            for b in range(B):
                mm = pe.transpose(ps[:, 2, 128 + b * M:128 + (b + 1) * M], ctx_rows[:, b, :], ident[0:M, 0:M])
            mm.then_inc(S("cols.turned"), 1)
            pe.wait_ge(S("inproj.loaded"), 32)
            for k in range(4):
                mm = pe.transpose(ps[:, 3, k * P:(k + 1) * P], in_proj[:, k, :], ident[:, :])
            mm.then_inc(S("wT.turned"), 1)
            pe.wait_ge(S("L0.z3"), 1)
            pe.wait_ge(S("L0.xT"), B)
            for b in range(B):
                mm = pe.matmul(ps[0:2, 4, :], z3[:, 1 - b:3 - b], half(xT, b), start=(b == 0), stop=(b == 1))
            mm.then_inc(S("L0.scores"), 1)
            pe.wait_ge(S("wT.made"), 1)
            pe.wait_ge(S("ctxT.made"), 1)
            pe.wait_ge(S("rows.loaded"), 16)
            pe.wait_ge(S("ctxw.loaded"), 16)
            ctx_w = [(wT[:, 1, :], wT[:, 2, :], "L0_bv"), (W["L1_xattn_WK2"], W["L1_xattn_WV2"], None),
                     (W["L2_xattn_ca_wk"], W["L2_xattn_ca_wv"], "L2_xattn_ca_bv"),
                     (W["L3_xattn_a2_wk"], W["L3_xattn_a2_wv"], None)]
            for layer, (wk, wv, bv) in enumerate(ctx_w):
                bank = (5, 6, 7, 0)[layer]
                pe.matmul(ps[:, bank, 0:B * M], wk, ctxT[:, :], start=True, stop=True)
                for b in range(B):
                    o = ps[0:M, bank, 160 + b * D:160 + (b + 1) * D]
                    mm = pe.matmul(o, ctxT[:, b * M:(b + 1) * M], wv, start=True, stop=bv is None)
                    if bv is not None:
                        mm = pe.matmul(o, ones_row[:, 0:M], row(bv), start=False, stop=True)
                mm.then_inc(S("ctx.mm"), 1)
            pe.wait_ge(S("ctx.k"), 3)
            pe.matmul(ps[:, 1, 0:B * M], swap[:, :], kc[:, 2, :], start=True, stop=True).then_inc(S("ctx.swapped"), 1)

            pe.wait_ge(S("L0.rank"), 1)
            for t in range(QB):
                mm = pe.transpose(ps[:, 4, t * B:(t + 1) * B], tokrank[:, t * P:(t + 1) * P], ident[0:2, 0:2])
            mm.then_inc(S("L0.rankT"), 1)
            pe.wait_ge(S("L0.onehot"), 1)
            for b in range(B):
                for t in range(QB):
                    mm = pe.matmul(ps[:, 3, b * TOPK:(b + 1) * TOPK], x[:, b * QB + t, :], onehot[:, b, t, :],
                                   start=(t == 0), stop=(t == QB - 1))
            mm.then_inc(S("L0.picked"), 1)
            for b in range(B):
                if b == 0:
                    pe.wait_ge(S("ctx.k"), 4)
                    pe.wait_ge(S("ctx.v"), 4)
                for t in range(QB):
                    mm = pe.transpose(ps[0:TOPK, 5 + b, t * P:(t + 1) * P], onehot[:, b, t, :], ident[:, :])
            mm.then_inc(S("L0.onehotT.mm"), 1)
            pe.wait_ge(S("L0.picked.sb"), 1)
            pe.matmul(ps[:, 4, 64:64 + B * TOPK], wT[:, 0, :], l0_xs[:, :], start=True, stop=True
                      ).then_inc(S("L0.q.mm"), 1)
            pe.wait_ge(S("L0.qblk"), 1)
            for b in range(B):
                for c in range(2):
                    mm = pe.matmul(ps[0:80, 7, (2 * b + c) * M:(2 * b + c + 1) * M],
                                   l0_qblk[:, b, c * 80:(c + 1) * 80], kc[:, 0, b * M:(b + 1) * M],
                                   start=True, stop=True)
            mm.then_inc(S("L0.s"), 1)
            pe.wait_ge(S("L0.p"), 1)
            for n in range(4):
                mm = pe.transpose(ps[0:M, 3, n * 80:(n + 1) * 80], l0_p[:, n, :], ident[0:80, 0:80])
            mm.then_inc(S("L0.t"), 1)
            pe.wait_ge(S("L0.pt"), 1)
            for b in range(B):
                mm = pe.matmul(ps[:, 4, b * 160:(b + 1) * 160], vc[:, 0, b, :], l0_pt[:, b * 160:(b + 1) * 160],
                               start=True, stop=True)
            mm.then_inc(S("L0.oT.mm"), 1)
            pe.wait_ge(S("L0.oT"), 1)
            for b in range(B):
                o = ps[0:TOPK, 7, b * D:(b + 1) * D]
                pe.matmul(o, l0_ot[:, b, :], wT[:, 3, :], start=True, stop=False)
                mm = pe.matmul(o, ones_row[:, 0:TOPK], row("L0_xattn_out_b"), start=False, stop=True)
            mm.then_inc(S("L0.ao.mm"), 1)
            pe.wait_ge(S("L0.ao"), 1)
            for b in range(B):
                for t in range(QB):
                    mm = pe.matmul(ps[:, 5 + b, t * P:(t + 1) * P], onehotT[:, b, t, :], l0_ao[:, b, :],
                                   start=True, stop=True)
                mm.then_inc(S("L0.put"), 1)

            pe.wait_ge(S("weights.loaded"), 16 * ((len(SQUARE) - 1) // SQUARE_LOAD))
            if stop >= 1:
                turn_state("L1.sa", x, "L0.x", QB)
                qkv("L1.sa", W["L1_xattn_WQ1"], W["L1_xattn_WK1"], W["L1_xattn_WV1"])
                pe.wait_ge(S("L1.sa.v"), B)
                single_attention("L1.sa", "L1.sa.qk", 2 * B, lambda i: kT[:, (i // QB) * N:(i // QB) * N + (i % QB + 1) * P],
                                 lambda i: (i % QB + 1) * P, lambda i, c: v_rows[:, (i // QB) * QB + c, :], True)
                turn_state("L1.ca", x, "L1.ln1.x")
                for k in range(B):
                    pe.wait_ge(S("state.T"), state("L1.ca", k))
                    project("L1.ca", W["L1_xattn_WQ2"], k, 2 + k).then_inc(S("L1.ca.q.mm"), 1)
                single_attention("L1.ca", "L1.ca.q", B, lambda i: kc[:, 1, (i // QB) * M:(i // QB + 1) * M],
                                 lambda i: M, lambda i, c: vc[:, 1, i // QB, :], False)
                turn_state("L1.ff", x, "L1.ln2.x")
                feed_forward("L1.ff", l1_w1, l1_w2, "L1_xattn_b_ff2")

            if stop >= 2:
                turn_state("L2.sa", xh, "L2.ln1.xh")
                qkv("L2.sa", W["L2_xattn_sa_wq"], W["L2_xattn_sa_wk"], W["L2_xattn_sa_wv"], "L2_xattn_sa_bv")
                for n, src in enumerate((qT, kT)):
                    for k in range(B):
                        pe.wait_ge(S("L2.sa.qk"), 2 * n + k + 1)
                        pe.matmul(ps[:, 2 * n + k, :], swap[:, :], half(src, k), start=True, stop=True
                                  ).then_inc(S("L2.sa.swapped"), 1)
                pe.wait_ge(S("L2.stacked"), 16 * 2 * B * len(TERMS))
                pe.wait_ge(S("stack.ones"), 3)
                pe.wait_ge(S("L2.sa.v"), B)

                def row_scores(u, p, first=False):
                    if not first:
                        pe.wait_ge(S("L2.max"), u - 1)
                    for qb in range(QB):
                        n = (qb + 1) * P
                        pe.matmul(ps[:, 4 * p + qb, 0:n], q_stack[0:STACK, bass.ds(u * N + qb * P, P)],
                                  k_stack[0:STACK, bass.ds(u * N, n)], start=True, stop=False)
                        mm = pe.matmul(ps[:, 4 * p + qb, n - P:n], ident16[:, :], hide_q[:, :], start=False, stop=True)
                    mm.then_inc(S("L2.s"), 1)

                for p in range(2):
                    row_scores(p, p, first=True)
                with pe.Fori(1, U // 2) as i:
                    for p in range(2):
                        row_scores(2 * i + p, p)
                pe.wait_ge(S("L2.max"), U)
                pe.transpose(ps[:, 0, 0:P], neg_max[:, :], ident[:, :]).then_inc(S("L2.maxT"), 1)
                pe.wait_ge(S("L2.shift.placed"), 32)

                def key_scores(u, p, first=False):
                    if not first:
                        pe.wait_ge(S("L2.exp"), u - 1)
                    for kb in (0, 1, 3, 2):
                        at = 3 * p * 512 + KEY_TILE_AT[kb]
                        n = N - kb * P
                        pe.matmul(ps_flat[:, at:at + n], k_stack[0:STACK, bass.ds(u * N + kb * P, P)],
                                  q_stack[0:STACK, bass.ds(u * N + kb * P, n)], start=True, stop=False)
                        mm = pe.matmul(ps_flat[:, at:at + P], ident16[:, :], hide_k[:, :], start=False, stop=True)
                    mm.then_inc(S("L2.st"), 1)

                def outputs(u, h, p, first=False):
                    pe.wait_ge(S("L2.exp"), u + 1)
                    for qb in range(QB):
                        for kb in range(qb + 1):
                            e = e_buf[:, p, KEY_TILE_AT[kb] + (qb - kb) * P:KEY_TILE_AT[kb] + (qb - kb + 1) * P]
                            o = ps[:, 6 + qb // 2, bass.ds((qb % 2) * H * (DH + 1) + h * (DH + 1), DH + 1)]
                            vv = v_one[:, kb, :, :].rearrange("p u d -> p (u d)")
                            mm = pe.matmul(o, e, vv[:, bass.ds(u * (DH + 1), DH + 1)],
                                           start=(kb == 0), stop=(kb == qb))
                    mm.then_inc(S("L2.pv"), 1)

                key_scores(0, 0, first=True)
                for b in range(B):
                    if b == 1:
                        pe.wait_ge(S("L2.ca0.rows"), 1)
                    for p in range(2):
                        key_scores(b * H + p + 1, 1 - p, first=(b == 0 and p == 0))
                        outputs(b * H + p, p, p)
                    with pe.Fori(1, H // 2 - b) as i:
                        for p in range(2):
                            key_scores(b * H + 2 * i + p + 1, 1 - p)
                            outputs(b * H + 2 * i + p, 2 * i + p, p)
                key_scores(U - 1, 1)
                outputs(U - 2, H - 2, 0)
                outputs(U - 1, H - 1, 1)
                out_project("L2.ca0", W["L2_xattn_sa_wo"], "L2_xattn_sa_bo", "L2.ca0.rows")
                turn_state("L2.ca", xh, "L2.ln2.xh")
                for k in range(B):
                    pe.wait_ge(S("state.T"), state("L2.ca", k))
                    project("L2.ca", W["L2_xattn_ca_wq"], k, 2 + k).then_inc(S("L2.ca.q.mm"), 1)
                for k in range(B):
                    pe.wait_ge(S("L2.ca.qraw"), k + 1)
                    pe.matmul(ps[:, 4 + k, :], swap[:, :], half(qT, k), start=True, stop=True
                              ).then_inc(S("L2.ca.swapped"), 1)
                pe.wait_ge(S("ctx.masked"), 4)
                cross("L2.ca", km2, lambda b: vc[:, 2, b, :], F32)
                out_project("L2.co", W["L2_xattn_ca_wo"], "L2_xattn_ca_bo", "L2.ca.rows", QB)
                turn_state("L2.ff", xh, "L2.ln3.xh")
                feed_forward("L2.ff", l2_w1, l2_w2, "L2_xattn_fc2_b")

            if stop >= 3:
                turn_state("L3.sa", xh, "L3.ln1.xh")
                qkv("L3.sa", W["L3_xattn_a1_wq"], W["L3_xattn_a1_wk"], W["L3_xattn_a1_wv"])
                pe.wait_ge(S("L3.ints"), 4 * B)
                for b in range(B):
                    for kb in range(2):
                        mm = pe.matmul(ps[:, 5, b * P:(b + 1) * P], c255[:, :], v_int[:, b * QB + kb, :],
                                       start=(kb == 0), stop=(kb == 1))
                mm.then_inc(S("L3.c255"), 1)
                pe.wait_ge(S("L3.c255.sb"), 1)

                def int_scores(b, u, qb, first=False):
                    if not first:
                        pe.wait_ge(S("L3.exp"), 4 * u + qb - 3)
                    pe.matmul(ps[:, qb, :], tile(q_int, b * QB + qb), k_stack[:, bass.ds(u * N, N)],
                              start=True, stop=True).then_inc(S("L3.s"), 1)

                def int_turn(u, p, kb, first=False):
                    if kb == 0:
                        pe.wait_ge(S("L3.rounded"), 4 * u + 4)
                    if kb >= 2:
                        pe.wait_ge(S("L3.pt.act"), 2 * u + kb - 1)
                    elif not first:
                        pe.wait_ge(S("L3.pt.dve"), 2 * u + kb - 1)
                    for qb in range(QB):
                        mm = pe.transpose(ps[:, 4 + kb % 2, qb * P:(qb + 1) * P],
                                          e_buf[:, p, qb * N + kb * P:qb * N + (kb + 1) * P], ident[:, :])
                    mm.then_inc(S("L3.t"), 1)

                def int_outputs(b, u, p, h):
                    pe.wait_ge(S("L3.pt.act"), 2 * u + 2)
                    pe.wait_ge(S("L3.pt.dve"), 2 * u + 2)
                    for qb in range(QB):
                        for kb in range(QB):
                            vv = v_neg if kb < 2 else v_int
                            mm = pe.matmul(ps[:, 6 + b, bass.ds(qb * P + h * DH, DH)],
                                           t_buf[:, p, kb * N + qb * P:kb * N + (qb + 1) * P],
                                           vv[:, b * QB + kb, bass.ds(h * DH, DH)],
                                           start=(kb == 0), stop=(kb == QB - 1))
                    mm.then_inc(S("L3.pv"), 1)

                pe.wait_ge(S("L3.kmask"), B)
                for qb in range(QB):
                    int_scores(0, 0, qb, first=True)
                for b in range(B):
                    def unit(b, u, h, p, next_b, first=False):
                        if next_b < B:
                            for qb in range(QB):
                                int_scores(next_b, u + 1, qb)
                        for kb in range(QB):
                            int_turn(u, p, kb, first)
                        int_outputs(b, u, p, h)

                    unit(b, b * H, 0, 0, b, first=(b == 0))
                    unit(b, b * H + 1, 1, 1, b)
                    with pe.Fori(1, H // 2 - 1) as i:
                        for p in range(2):
                            unit(b, b * H + 2 * i + p, 2 * i + p, p, b)
                    unit(b, b * H + H - 2, H - 2, 0, b)
                    unit(b, b * H + H - 1, H - 1, 1, b + 1)
                out_project("L3.ca0", W["L3_xattn_a1_wo"], "L3_xattn_a1_bo", "L3.ca0.rows")
                turn_state("L3.ca", xh, "L3.ln2.xh")
                for k in range(B):
                    pe.wait_ge(S("state.T"), state("L3.ca", k))
                    project("L3.ca", W["L3_xattn_a2_wq"], k, 2 + k).then_inc(S("L3.ca.q.mm"), 1)
                cross("L3.ca", km3, lambda b: vc3[:, b, :], BF16)
                out_project("L3.co", W["L3_xattn_a2_wo"], "L3_xattn_a2_bo", "L3.ca.rows", QB)
                turn_state("L3.ff", xh, "L3.ln3.xh")
                feed_forward("L3.ff", l3_w1, l3_w2, "L3_xattn_ff_b2", gated=True)


        @block.scalar
        def _(act):
            def copy(o, i, sem):
                act.activation(o, i, ACT.Copy).then_inc(S(sem), 1)

            def state_out(name, g=None, b=None):
                for k in range(B):
                    act.wait_ge(S("state.turned"), state(name, k))
                    if g is None:
                        copy(half(xT, k), ps[:, k, :], "state.T")
                    else:
                        act.activation(half(xT, k), ps[:, k, :], ACT.Identity, scale=g, bias=b
                                       ).then_inc(S("state.T"), 1)

            def project_out(dst, mm, bank, sem, bias=None):
                for k in range(B):
                    act.wait_ge(S(mm), k + 1)
                    if bias is None:
                        copy(half(dst, k), ps[:, bank + k, :], sem)
                    else:
                        act.activation(half(dst, k), ps[:, bank + k, :], ACT.Identity, bias=bias).then_inc(S(sem), 1)

            def single_attention(name, width):
                for i in range(T + 1):
                    if i < T:
                        act.wait_ge(S("one.m"), count(name, "m") + i + 1)
                        if i >= 2:
                            act.wait_ge(S("one.t"), count(name, "t") + i - 1)
                        act.activation(e_buf[:, i % 2, 0:width(i)], ps[:, 2 + i % 2, 0:width(i)], ACT.Exp,
                                       bias=stats[:, 1, i:i + 1], scale=ONE_SCALE, accum_out=stats[:, 2, i:i + 1]
                                       ).then_inc(S("one.exp"), 1)
                    if i >= 1:
                        j = i - 1
                        act.wait_ge(S("one.t"), count(name, "t") + j + 1)
                        if j >= 2:
                            act.wait_ge(S("one.o"), count(name, "o") + j - 1)
                        r, n = min(P, width(j)), max(P, width(j))
                        copy(pt_buf[0:r, j % 2, 0:n], ps[0:r, 4 + j % 2, 0:n], "one.pt")

            def hidden(name, func, bias):
                for n in range(B * FC):
                    k, c = divmod(n, FC)
                    act.wait_ge(S("ff.h"), count(name, "h") + n + 1)
                    act.activation(half(hid[:, c, :], k), ps[:, HIDDEN[n % 4], :], func, bias=col(bias, c)
                                   ).then_inc(S("ff.hid"), 1)

            def cross(name, quantised):
                for i in range(T + 1):
                    if quantised and i >= 1:
                        act.wait_ge(S("cross.mul"), i)
                        e = e_buf[:, (i - 1) % 2, 0:H * M]
                        act.activation(e, e, ACT.Identity, bias=magic_col[:, :]).then_inc(S("cross.p"), 1)
                    if i < T:
                        act.wait_ge(S("cross.sub"), count(name, "sub") + i + 1)
                        e = e_buf[:, i % 2, 0:H * M]
                        if quantised:
                            act.activation(e, e, ACT.Exp, scale=sders[:, 9:10]).then_inc(S("cross.exp"), 1)
                        else:
                            act.activation(e, e, ACT.Exp).then_inc(S("cross.p"), 1)
                    if not quantised and i >= 1:
                        for c in range(4):
                            n = 4 * (i - 1) + c
                            act.wait_ge(S("cross.t"), count(name, "t") + n + 1)
                            if n >= 2:
                                act.wait_ge(S("cross.o"), count(name, "o") + n - 1)
                            copy(pt_buf[0:M, c % 2, :], ps[0:M, 3 + c % 2, :], "cross.pt")

            for k in range(B):
                act.wait_ge(S("L0.turned"), k + 1)
                copy(half(xT, k), ps[:, k, :], "L0.xT")
            act.wait_ge(S("wT.turned"), 1)
            copy(wT[:, :, :].rearrange("p t d -> p (t d)"), ps[:, 3, :], "wT.made")
            act.wait_ge(S("cols.made"), 1)
            for layer, bias in enumerate((col("L0_xattn_in_proj_b", 1), None, col("L2_xattn_ca_bk"), None)):
                act.wait_ge(S("ctx.mm"), layer + 1)
                src = ps[:, (5, 6, 7, 0)[layer], 0:B * M]
                if bias is None:
                    copy(kc[:, layer, :], src, "ctx.k")
                else:
                    act.activation(kc[:, layer, :], src, ACT.Identity, bias=bias).then_inc(S("ctx.k"), 1)
            act.wait_ge(S("L0.picked"), 1)
            copy(l0_xs[:, :], ps[:, 3, 0:B * TOPK], "L0.picked.sb")
            act.wait_ge(S("L0.sub"), 1)
            act.activation(l0_p, l0_p, ACT.Exp, scale=HEAD_SCALE).then_inc(S("L0.exp"), 1)
            act.wait_ge(S("L0.t"), 1)
            copy(l0_pt, ps[0:M, 3, 0:B * 160], "L0.pt")
            act.wait_ge(S("L0.ao.mm"), 1)
            copy(l0_ao[:, :, :].rearrange("p b d -> p (b d)"), ps[0:TOPK, 7, 0:B * D], "L0.ao")

            if stop >= 1:
                state_out("L1.sa")
                project_out(qT, "L1.sa.q.mm", 2, "L1.sa.qk")
                project_out(kT, "L1.sa.k.mm", 4, "L1.sa.qk")
                single_attention("L1.sa", lambda i: (i % QB + 1) * P)
                state_out("L1.ca")
                project_out(qT, "L1.ca.q.mm", 2, "L1.ca.q")
                single_attention("L1.ca", lambda i: M)
                state_out("L1.ff")
                hidden("L1.ff", ACT.Relu, "L1_xattn_b_ff1")
            if stop >= 2:
                state_out("L2.sa", col("L2_xattn_ln1_g"), col("L2_xattn_ln1_b"))
                project_out(qT, "L2.sa.q.mm", 2, "L2.sa.qk", col("L2_xattn_sa_bq"))
                project_out(kT, "L2.sa.k.mm", 4, "L2.sa.qk", col("L2_xattn_sa_bk"))
                for side, name in enumerate(("q", "k")):
                    act.wait_ge(S("L2.sa.rope"), B * (side + 1))
                    copy(parts[:, side, 0, :], ta[:, :], f"L2.{name}.parts")
                    act.wait_ge(S("L2.rest"), side + 1)
                    copy(parts[:, side, 1, :], tb[:, :], f"L2.{name}.parts")

                def exps(u, p, first=False):
                    act.wait_ge(S("L2.st"), u + 1)
                    if not first:
                        act.wait_ge(S("L2.pv"), u - 1)
                    act.activation(e_buf[:, p, 0:CAUSAL_COLS], ps_flat[:, 3 * p * 512:3 * p * 512 + CAUSAL_COLS],
                                   ACT.Exp).then_inc(S("L2.exp"), 1)
                for p in range(2):
                    exps(p, p, first=True)
                with act.Fori(1, U // 2) as i:
                    for p in range(2):
                        exps(2 * i + p, p)
                state_out("L2.ca0")
                state_out("L2.ca", col("L2_xattn_ln2_g"), col("L2_xattn_ln2_b"))
                project_out(qT, "L2.ca.q.mm", 2, "L2.ca.qraw", col("L2_xattn_ca_bq"))
                cross("L2.ca", False)
                state_out("L2.co")
                state_out("L2.ff", col("L2_xattn_ln3_g"), col("L2_xattn_ln3_b"))
                hidden("L2.ff", ACT.Gelu_apprx_tanh, "L2_xattn_fc1_b")
            if stop >= 3:
                state_out("L3.sa", col("L3_xattn_ln1_g"), col("L3_xattn_ln1_b"))
                act.wait_ge(S("L3.c255"), 1)
                copy(cv[:, :, :].rearrange("p b d -> p (b d)"), ps[:, 5, 0:B * P], "L3.c255.sb")

                def exps3(u, p, first=False):
                    for qb in range(QB):
                        act.wait_ge(S("L3.m"), 2 * u + qb // 2 + 1)
                        if qb == 0 and not first:
                            act.wait_ge(S("L3.t"), 4 * u - 4)
                        act.activation(e_buf[:, p, qb * N:(qb + 1) * N], ps[:, qb, :], ACT.Exp,
                                       bias=stats[:, 2 + p, qb:qb + 1], scale=sders[:, 8:9],
                                       accum_out=stats[:, 6 + p, qb:qb + 1]).then_inc(S("L3.exp"), 1)

                def turned3(u, p, first=False):
                    for kb in range(2):
                        act.wait_ge(S("L3.t"), 4 * u + kb + 1)
                        if kb == 0 and not first:
                            act.wait_ge(S("L3.pv"), u - 1)
                        act.activation(t_buf[:, p, kb * N:(kb + 1) * N], ps[:, 4 + kb, :], ACT.Relu,
                                       bias=relu_top[:, :], scale=-1.0).then_inc(S("L3.pt.act"), 1)
                exps3(0, 0, True)
                exps3(1, 1, True)
                turned3(0, 0, True)
                exps3(2, 0)
                turned3(1, 1, True)
                exps3(3, 1)
                with act.Fori(2, U // 2) as i:
                    for p in range(2):
                        turned3(2 * i + p - 2, p)
                        exps3(2 * i + p, p)
                turned3(U - 2, 0)
                turned3(U - 1, 1)
                state_out("L3.ca0")
                state_out("L3.ca", col("L3_xattn_ln2_g"), col("L3_xattn_ln2_b"))
                cross("L3.ca", True)
                state_out("L3.co")
                state_out("L3.ff", col("L3_xattn_ln3_g"), col("L3_xattn_ln3_b"))
                for n in range(B * FC):
                    c = n % FC
                    act.wait_ge(S("L3.ff.h"), count("L3.ff", "h") + n + 1)
                    if n >= 2:
                        act.wait_ge(S("L3.ff.hid"), count("L3.ff", "hid") + n - 1)
                    act.activation(gel[:, n % 2, :], ps[:, HIDDEN[2 * (n % 2) + 1], :], ACT.Gelu,
                                   bias=col("L3_xattn_ff_b1", FC + c)).then_inc(S("L3.ff.gel"), 1)

        @block.vector
        def _(dve):
            own = [0]

            def then(ins):
                own[0] += 1
                ins.then_inc(S("dve.own"), 1)
                dve.wait_ge(S("dve.own"), own[0])

            def norm(name, ready, each, to=None):
                at = B * ln_index[name]
                for k in range(B):
                    dve.wait_ge(S(ready), count(*ready.rsplit(".", 1)) + each * (k + 1))
                    for t in range(k * QB, (k + 1) * QB):
                        ins = dve.bn_stats(st[:, t, :], x[:, t, :])
                    then(ins)
                    for t in range(k * QB, (k + 1) * QB):
                        ins = dve.bn_aggr(mv[:, t, :], st[:, t, :])
                    ins.then_inc(S("ln.mv"), 1)
                for k in range(B):
                    dve.wait_ge(S("ln.rstd"), at + k + 1)
                    for t in range(k * QB, (k + 1) * QB):
                        ins = dve.tensor_scalar(xh[:, t, :], x[:, t, :], mv[:, t, 0:1], rstd[:, t:t + 1],
                                                ALU.subtract, ALU.mult)
                    if to is None:
                        ins.then_inc(S(f"{name}.xh"), 1)
                    else:
                        then(ins)
                        dve.tensor_tensor(half_rows(xh, k), half_rows(xh, k),
                                          spread[:, to, :].unsqueeze(1).broadcast_to([P, QB, D]), ALU.mult
                                          ).then_inc(S(f"{name}.scaled"), 1)

            def add_to_x(name, bank):
                for k in range(B):
                    dve.wait_ge(S(f"{name}.o"), count(name, "o") + k + 1)
                    dve.tensor_tensor(half_rows(x, k), bank_rows(bank + k), half_rows(x, k), ALU.add
                                      ).then_inc(S(f"{name}.x"), 1)

            def single_attention(name, width):
                for i in range(T + 2):
                    if i < T:
                        dve.wait_ge(S("one.s"), count(name, "s") + i + 1)
                        then(dve.tensor_reduce(stats[:, 0, i:i + 1], ps[:, 2 + i % 2, 0:width(i)], AX, ALU.max,
                                               negate=True))
                        dve.tensor_scalar(stats[:, 1, i:i + 1], stats[:, 0, i:i + 1], ONE_SCALE, None, ALU.mult
                                          ).then_inc(S("one.m"), 1)
                    if i >= 2:
                        j = i - 2
                        dve.wait_ge(S("one.exp"), count(name, "exp") + j + 1)
                        then(dve.reciprocal(stats[:, 3, j:j + 1], stats[:, 2, j:j + 1]))
                        dve.wait_ge(S("one.o"), count(name, "o") + j + 1)
                        dve.scalar_tensor_tensor(x[:, j, :], ps[:, 6 + j % 2, 0:P], stats[:, 3, j:j + 1], x[:, j, :],
                                                 ALU.mult, ALU.add).then_inc(S("one.x"), 1)

            def rotate(dst, raw, swapped, scale, sem, cos=cos_t, sin=sin_t):
                a, b = half_of(dst, ta), half_of(dst, tb)
                dve.scalar_tensor_tensor(a, raw, scale, cos[:, :], ALU.mult, ALU.mult)
                then(dve.scalar_tensor_tensor(b, swapped, scale, sin[:, :], ALU.mult, ALU.mult))
                dve.tensor_tensor(half(dst[0], dst[1]), a, b, ALU.add).then_inc(S(sem), 1)

            def half_of(dst, buf):
                return half(buf, dst[1])

            def quantise(dst, src, tmp, recip_step):
                then(dve.tensor_scalar(tmp, src, recip_step, MAGIC, ALU.mult, ALU.add))
                then(dve.tensor_scalar(tmp, tmp, MAGIC - ZERO_POINT, MAGIC + QMAX - ZERO_POINT, ALU.max, ALU.min))
                return dve.tensor_scalar(dst, tmp, MAGIC, None, ALU.subtract)

            def cross(name, quantised):
                def finish(i):
                    p = i % 2
                    e = e_buf[:, p, 0:H * M].rearrange("p (h m) -> p h m", m=M)
                    dve.wait_ge(S("cross.exp" if quantised else "cross.p"), i + 1)
                    then(dve.tensor_reduce(cr_sum[:, p, :], e, AX, ALU.add))
                    if quantised:
                        then(dve.tensor_scalar(cr_sum[:, p, :], cr_sum[:, p, :], sc(DW2), None, ALU.mult))
                    then(dve.reciprocal(cr_rec[:, p, :], cr_sum[:, p, :]))
                    if quantised:
                        dve.tensor_tensor(e, e, cr_rec[:, p, :].unsqueeze(2).broadcast_to([P, H, M]), ALU.mult
                                          ).then_inc(S("cross.mul"), 1)

                def start(i):
                    p = i % 2
                    dve.wait_ge(S("cross.s"), count(name, "s") + i + 1)
                    for g, (h0, n) in enumerate(CROSS_GROUPS):
                        s = ps[:, g, 0:n * M].rearrange("p (h m) -> p h m", m=M)
                        ins = dve.tensor_reduce(cr_max[:, p, h0:h0 + n], s, AX, ALU.max)
                    then(ins)
                    if i >= 2:
                        dve.wait_ge(S("cross.t"), count(name, "t") + 4 * (i - 1))
                    for g, (h0, n) in enumerate(CROSS_GROUPS):
                        s = ps[:, g, 0:n * M].rearrange("p (h m) -> p h m", m=M)
                        e = e_buf[:, p, h0 * M:(h0 + n) * M].rearrange("p (h m) -> p h m", m=M)
                        ins = dve.tensor_tensor(e, s, cr_max[:, p, h0:h0 + n].unsqueeze(2).broadcast_to([P, n, M]),
                                                ALU.subtract)
                    ins.then_inc(S("cross.sub"), 1)

                for i in range(T + 1):
                    if i >= 1:
                        finish(i - 1)
                    if i < T:
                        start(i)
                    if i >= 1:
                        j = i - 1
                        if quantised:
                            for c in range(4):
                                n = 4 * j + c
                                dve.wait_ge(S("cross.t"), count(name, "t") + n + 1)
                                if n >= 2:
                                    dve.wait_ge(S("cross.o"), count(name, "o") + n - 1)
                                dve.tensor_scalar(t_buf[0:M, c % 2, 0:N], ps[0:M, 3 + c % 2, :], MAGIC, QMAX,
                                                  ALU.subtract, ALU.min).then_inc(S("cross.pt"), 1)
                        dve.wait_ge(S("cross.o"), count(name, "o") + 4 * (j + 1))
                        o = ps[:, 6 + j % 2, 0:P]
                        if quantised:
                            ins = dve.tensor_scalar(xh[:, j, :], o, sders[:, 11:12], None, ALU.mult)
                        else:
                            ins = dve.tensor_tensor(xh[:, j, :].rearrange("p (h d) -> p h d", d=DH),
                                                    o.rearrange("p (h d) -> p h d", d=DH),
                                                    cr_rec[:, j % 2, :].unsqueeze(2).broadcast_to([P, H, DH]),
                                                    ALU.mult)
                        ins.then_inc(S("cross.rows"), 1)

            dve.memset(magic_col[:, :], MAGIC)
            dve.memset(z3[:, :], 0.0)
            then(dve.memset(l0_zero, 0.0))
            dve.wait_ge(S("cols.turned"), 3)
            dve.tensor_copy(cols[:, :], ps[:, 2, 0:NCOL]).then_inc(S("cols.made"), 1)
            then(dve.tensor_copy(scalars[:, :], ps[:, 2, 64:73]))
            dve.tensor_copy(ctxT[:, :], ps[:, 2, 128:128 + B * M]).then_inc(S("ctxT.made"), 1)
            dve.wait_ge(S("cols.made"), 1)
            dve.tensor_copy(z3[:, 1:2], col("L0_xattn_score_w")).then_inc(S("L0.z3"), 1)
            dve.reciprocal(sders[:, 0:8], scalars[:, 0:8])
            for k in range(2):
                dve.scalar_tensor_tensor(sders[:, 8 + k:9 + k], sc(4 * k), HEAD_SCALE, sc(4 * k + 1),
                                         ALU.mult, ALU.mult)
                ins = dve.tensor_tensor(sders[:, 10 + k:11 + k], sc(4 * k + 2), sc(4 * k + 3), ALU.mult)
            then(ins)

            dve.wait_ge(S("L0.scores"), 1)
            then(dve.tensor_scalar(l0_sc, ps[0:2, 4, :], scalars[0:2, SCORE_B:SCORE_B + 1], None, ALU.add))
            then(dve.max(l0_best[:, :], l0_sc))
            then(dve.match_replace(l0_left, l0_best[:, :], l0_sc, TAKEN))
            then(dve.max(l0_next[:, :], l0_left))
            then(dve.memset(l0_next[:, TOPK - 8:8], TAKEN))
            then(dve.match_replace(l0_sc, l0_next[:, :], l0_left, TAKEN))
            then(dve.tensor_scalar(l0_sc, l0_sc, TAKEN, None, ALU.is_equal))
            then(dve.tensor_tensor_scan(l0_left, l0_sc, l0_zero, 0.0, ALU.add, ALU.add))
            dve.tensor_tensor(tokrank, l0_left, l0_sc, ALU.mult).then_inc(S("L0.rank"), 1)

            for layer in range(4):
                dve.wait_ge(S("ctx.k"), layer + 1)
                dve.tensor_copy(vc[:, layer, :, :].rearrange("p b d -> p (b d)"),
                                ps[0:M, (5, 6, 7, 0)[layer], 160:160 + B * D]).then_inc(S("ctx.v"), 1)
            dve.wait_ge(S("L0.rankT"), 1)
            for b in range(B):
                r = ps[:, 4, 0:QB * B].rearrange("p (t b) -> p t b", b=B)[:, :, b]
                ins = dve.tensor_tensor(onehot[:, b, :, :], r.unsqueeze(2).broadcast_to([P, QB, TOPK]),
                                        ranks[:, :].unsqueeze(1).broadcast_to([P, QB, TOPK]), ALU.is_equal)
            ins.then_inc(S("L0.onehot"), 1)
            dve.wait_ge(S("L0.onehot"), 1)
            then(dve.tensor_reduce(kept[:, :], onehot[:, :, :, :].rearrange("p b t r -> p (b t) r"), AX, ALU.add))
            then(dve.tensor_scalar(kept[:, :], kept[:, :], -1.0, 1.0, ALU.mult, ALU.add))
            dve.wait_ge(S("L0.onehotT.mm"), 1)
            for b in range(B):
                ins = dve.tensor_copy(onehotT[:, b, :, :].rearrange("p t n -> p (t n)"), ps[0:TOPK, 5 + b, :])
            then(ins)
            dve.wait_ge(S("L0.q.mm"), 1)
            then(dve.tensor_scalar(l0_q[:, :], ps[:, 4, 64:64 + B * TOPK], col("L0_xattn_in_proj_b"), None, ALU.add))
            for b in range(B):
                ins = dve.tensor_tensor(
                    l0_qblk[:, b, :].rearrange("p (h q) -> p h q", q=TOPK),
                    l0_q[:, b * TOPK:(b + 1) * TOPK].unsqueeze(1).broadcast_to([P, H, TOPK]),
                    head_mask[:, :].unsqueeze(2).broadcast_to([P, H, TOPK]), ALU.mult)
            ins.then_inc(S("L0.qblk"), 1)

            dve.wait_ge(S("rope.loaded"), 32)
            dve.wait_ge(S("ctx.swapped"), 1)
            c3, s3 = (a[:, 0:M].unsqueeze(1).broadcast_to([P, B, M]) for a in (cos_t, sin_t))
            kc2 = kc[:, 2, :].rearrange("p (b m) -> p b m", b=B)
            ta2, tb2 = (a[:, 0:B * M].rearrange("p (b m) -> p b m", b=B) for a in (ta, tb))
            dve.tensor_tensor(ta2, kc2, c3, ALU.mult)
            then(dve.tensor_tensor(tb2, ps[:, 1, 0:B * M].rearrange("p (b m) -> p b m", b=B), s3, ALU.mult))
            dve.tensor_tensor(kc2, ta2, tb2, ALU.add).then_inc(S("ctx.rope"), 1)
            dve.wait_ge(S("ctx.rope"), 1)
            dve.wait_ge(S("ctx.k"), 4)
            quantise(kc[:, 3, :], kc[:, 3, :], ta[:, 0:B * M], sders[:, DK2:DK2 + 1]).then_inc(S("ctx.quant"), 1)
            dve.wait_ge(S("ctx.v"), 4)
            quantise(vc3[:, :, :].rearrange("p b d -> p (b d)"), vc[:, 3, :, :].rearrange("p b d -> p (b d)"),
                     tb[0:M, 0:B * D], sders[0:M, DV2:DV2 + 1]).then_inc(S("ctx.quant"), 1)

            dve.wait_ge(S("L0.s"), 1)
            s = ps[0:80, 7, 0:4 * M].rearrange("p (n m) -> p n m", m=M)
            then(dve.tensor_reduce(l0_st[:, 0, :], s, AX, ALU.max))
            dve.tensor_tensor(l0_p, s, l0_st[:, 0, :].unsqueeze(2).broadcast_to([80, 4, M]), ALU.subtract
                              ).then_inc(S("L0.sub"), 1)
            dve.wait_ge(S("L0.exp"), 1)
            then(dve.tensor_reduce(l0_st[:, 1, :], l0_p, AX, ALU.add))
            then(dve.reciprocal(l0_st[:, 2, :], l0_st[:, 1, :]))
            dve.tensor_tensor(l0_p, l0_p, l0_st[:, 2, :].unsqueeze(2).broadcast_to([80, 4, M]),
                              ALU.mult).then_inc(S("L0.p"), 1)
            dve.wait_ge(S("L0.oT.mm"), 1)
            for b in range(B):
                ins = dve.tensor_tensor(l0_od[:, b, :, :],
                                        ps[:, 4, b * 160:(b + 1) * 160].rearrange("p (h q) -> p h q", q=TOPK),
                                        head_mask[:, :].unsqueeze(2).broadcast_to([P, H, TOPK]), ALU.mult)
            then(ins)
            dve.tensor_reduce(l0_ot[:, :, :], l0_od[:, :, :, :].rearrange("p b h q -> p b q h"), AX, ALU.add
                              ).then_inc(S("L0.oT"), 1)
            for b in range(B):
                dve.wait_ge(S("L0.put"), b + 1)
                for t in range(QB):
                    n = b * QB + t
                    dve.scalar_tensor_tensor(x[:, n, :], x[:, n, :], kept[:, n:n + 1], ps[:, 5 + b, t * P:(t + 1) * P],
                                             ALU.mult, ALU.add).then_inc(S("L0.x"), 1)

            def values_out(name, dst):
                for k in range(B):
                    dve.wait_ge(S(f"{name}.v.mm"), k + 1)
                    dve.tensor_copy(dst(k), ps[:, 6 + k, :]).then_inc(S(f"{name}.v"), 1)

            if stop >= 1:
                for k in range(B):
                    dve.wait_ge(S("L1.sa.v.mm"), k + 1)
                    dve.tensor_copy(half_rows(v_rows, k), bank_rows(6 + k)).then_inc(S("L1.sa.v"), 1)
                dve.wait_ge(S("spread.loaded"), 16)
                single_attention("L1.sa", lambda i: (i % QB + 1) * P)
                norm("L1.ln1", "L1.sa.x", QB, to=0)
                dve.wait_ge(S("L1.ln1.x"), count("L1.ln1", "x") + B)
                single_attention("L1.ca", lambda i: M)
                norm("L1.ln2", "L1.ca.x", QB, to=2)
                dve.wait_ge(S("L1.ln2.x"), count("L1.ln2", "x") + B)
                add_to_x("L1.ff", 4)
                norm("L1.ln3", "L1.ff.x", 1, to=4)

            if stop >= 2:
                norm("L2.ln1", "L1.ln3.x", 1)
                dve.wait_ge(S("rope.loaded"), 32)
                for side, (src, scale, name) in enumerate(((qT, HEAD_SCALE, "q"), (kT, 1.0, "k"))):
                    if side == 1:
                        dve.wait_ge(S("L2.q.parts"), 3)
                    for k in range(B):
                        dve.wait_ge(S("L2.sa.swapped"), 2 * side + k + 1)
                        rotate((ta, k), half(src, k), ps[:, 2 * side + k, :],
                               scale, "L2.sa.rope")
                    dve.wait_ge(S(f"L2.{name}.parts"), 1)
                    dve.tensor_tensor(tb[:, :], ta[:, :], parts[:, side, 0, :], ALU.subtract
                                      ).then_inc(S("L2.rest"), 1)
                    dve.wait_ge(S("L2.rest"), side + 1)
                    dve.wait_ge(S(f"L2.{name}.parts"), 2)
                    dve.tensor_tensor(parts[:, side, 2, :], tb[:, :], parts[:, side, 1, :], ALU.subtract
                                      ).then_inc(S(f"L2.{name}.parts"), 1)
                    if side == 0:
                        for k in range(B):
                            dve.wait_ge(S("L2.sa.v.mm"), k + 1)
                            dve.tensor_copy(v_one[:, :, k * H:(k + 1) * H, 0:DH],
                                            ps[:, 6 + k, :].rearrange("p (t h d) -> p t h d", h=H, d=DH)
                                            ).then_inc(S("L2.sa.v"), 1)

                def maxima(u, p):
                    dve.wait_ge(S("L2.s"), u + 1)
                    for qb in range(QB):
                        ins = dve.tensor_reduce(neg_max[:, bass.ds(u * QB + qb, 1)], ps[:, 4 * p + qb, 0:(qb + 1) * P],
                                                AX, ALU.max, negate=True)
                    ins.then_inc(S("L2.max"), 1)
                with dve.Fori(0, U // 2) as i:
                    for p in range(2):
                        maxima(2 * i + p, p)
                dve.wait_ge(S("L2.maxT"), 1)
                dve.tensor_copy(shift[:, 0, :], ps[:, 0, 0:P]).then_inc(S("L2.shift"), 1)
                dve.wait_ge(S("L2.shift"), 1)
                dve.tensor_tensor(shift[:, 1, :], ps[:, 0, 0:P], shift[:, 0, :], ALU.subtract
                                  ).then_inc(S("L2.shift"), 1)
                for b in range(B):
                    dve.wait_ge(S("L2.pv"), H * (b + 1))
                    o = [ps[:, 6 + g, 0:2 * H * (DH + 1)].rearrange("p (t h d) -> p t h d", h=H, d=DH + 1)
                         for g in range(2)]
                    for g in range(2):
                        ins = dve.reciprocal(row_recip[:, 2 * g:2 * g + 2, :], o[g][:, :, :, DH])
                    then(ins)
                    for g in range(2):
                        t = b * QB + 2 * g
                        ins = dve.tensor_tensor(
                            xh[:, t:t + 2, :].rearrange("p t (h d) -> p t h d", d=DH), o[g][:, :, :, 0:DH],
                            row_recip[:, 2 * g:2 * g + 2, :].unsqueeze(3).broadcast_to([P, 2, H, DH]), ALU.mult)
                    ins.then_inc(S("L2.ca0.rows"), 1)
                add_to_x("L2.ca0", 2)
                norm("L2.ln2", "L2.ca0.x", 1)
                for k in range(B):
                    dve.wait_ge(S("L2.ca.swapped"), k + 1)
                    rotate((qT, k), half(qT, k), ps[:, 4 + k, :], HEAD_SCALE, "L2.ca.q")
                cross("L2.ca", False)
                add_to_x("L2.co", 2)
                norm("L2.ln3", "L2.co.x", 1)
                add_to_x("L2.ff", 4)

            if stop >= 3:
                norm("L3.ln1", "L2.ff.x", 1)
                for k in range(B):
                    dve.wait_ge(S("L3.sa.q.mm"), k + 1)
                    quantise(half(q_int, k), ps[:, 2 + k, :], half(ta, k), sders[:, DQ1:DQ1 + 1]
                             ).then_inc(S("L3.ints"), 1)
                    dve.wait_ge(S("L3.sa.k.mm"), k + 1)
                    quantise(half(k_int, k), ps[:, 4 + k, :], half(tb, k), sders[:, DK1:DK1 + 1]
                             ).then_inc(S("L3.ints"), 1)
                    dve.wait_ge(S("L3.sa.v.mm"), k + 1)
                    quantise(half_rows(v_int, k).rearrange("p t d -> p (t d)"), ps[:, 6 + k, :], gel[:, k, :],
                             sders[:, DV1:DV1 + 1]).then_inc(S("L3.ints"), 1)
                    dve.wait_ge(S("L3.ints"), 4 * k + 3)
                    dve.tensor_scalar(half_rows(v_neg, k), half_rows(v_int, k), -1.0, None, ALU.mult
                                      ).then_inc(S("L3.ints"), 1)
                for b in range(B):
                    for h in range(H):
                        u = b * H + h
                        ins = dve.tensor_scalar(k_stack[:, u * N:(u + 1) * N], half(k_int, b), head_mask[:, h:h + 1],
                                                None, ALU.mult)
                    ins.then_inc(S("L3.kmask"), 1)

                def maxima3(u, p):
                    for j in range(2):
                        dve.wait_ge(S("L3.s"), 4 * u + 2 * j + 2)
                        dve.tensor_reduce(stats[:, p, 2 * j:2 * j + 2], ps[:, 2 * j:2 * j + 2, :], AX, ALU.max,
                                          negate=True).then_inc(S("L3.nm"), 1)
                        dve.wait_ge(S("L3.nm"), 2 * u + j + 1)
                        dve.tensor_scalar(stats[:, 2 + p, 2 * j:2 * j + 2], stats[:, p, 2 * j:2 * j + 2],
                                          sders[:, 8:9], None, ALU.mult).then_inc(S("L3.m"), 1)

                def recips3(u, p):
                    dve.wait_ge(S("L3.exp"), 4 * u + 4)
                    dve.tensor_scalar(stats[:, 6 + p, 0:QB], stats[:, 6 + p, 0:QB], sc(DW1), None, ALU.mult
                                      ).then_inc(S("L3.sumdw"), 1)
                    dve.wait_ge(S("L3.sumdw"), u + 1)
                    dve.reciprocal(stats[:, 4 + p, 0:QB], stats[:, 6 + p, 0:QB]).then_inc(S("L3.recip"), 1)

                def turned3(u, p, first=False):
                    for kb in range(2, 4):
                        dve.wait_ge(S("L3.t"), 4 * u + kb + 1)
                        if kb == 2 and not first:
                            dve.wait_ge(S("L3.pv"), u - 1)
                        dve.tensor_scalar(t_buf[:, p, kb * N:(kb + 1) * N], ps[:, 2 + kb, :], MAGIC, QMAX,
                                          ALU.subtract, ALU.min).then_inc(S("L3.pt.dve"), 1)

                def rows3(b):
                    dve.wait_ge(S("L3.pv"), H * (b + 1))
                    then(dve.tensor_tensor(half_rows(xh, b), bank_rows(6 + b),
                                           cv[:, b, :].unsqueeze(1).broadcast_to([P, QB, D]), ALU.add))
                    dve.tensor_scalar(half_rows(xh, b), half_rows(xh, b), sders[:, 10:11], None, ALU.mult
                                      ).then_inc(S("L3.ca0.rows"), 1)

                maxima3(0, 0)
                recips3(0, 0)
                maxima3(1, 1)
                turned3(0, 0, True)
                recips3(1, 1)
                maxima3(2, 0)
                turned3(1, 1, True)
                recips3(2, 0)
                maxima3(3, 1)
                turned3(2, 0)
                recips3(3, 1)
                with dve.Fori(2, U // 2) as i:
                    for p in range(2):
                        maxima3(2 * i + p, p)
                        turned3(2 * i + p - 1, 1 - p)
                        recips3(2 * i + p, p)
                turned3(U - 1, 1)
                dve.wait_ge(S("L3.c255.sb"), 1)
                for b in range(B):
                    rows3(b)
                add_to_x("L3.ca0", 2)
                norm("L3.ln2", "L3.ca0.x", 1)
                for k in range(B):
                    dve.wait_ge(S("L3.ca.q.mm"), k + 1)
                    quantise(half(q_int, k), ps[:, 2 + k, :], half(ta, k), sders[:, DQ2:DQ2 + 1]
                             ).then_inc(S("L3.ca.q"), 1)
                cross("L3.ca", True)
                add_to_x("L3.co", 2)
                norm("L3.ln3", "L3.co.x", 1)
                for n in range(B * FC):
                    k, c = divmod(n, FC)
                    dve.wait_ge(S("L3.ff.gel"), n + 1)
                    dve.scalar_tensor_tensor(half(hid[:, c, :], k), ps[:, HIDDEN[2 * (n % 2)], :], col("L3_xattn_ff_b1", c),
                                             gel[:, n % 2, :], ALU.add, ALU.mult).then_inc(S("L3.ff.hid"), 1)
                add_to_x("L3.ff", 4)


def kernel(**inputs):
    import concourse.bacc as bacc
    from concourse.bass_utils import run_bass_kernel_spmd as run

    nc = bacc.Bacc("TRN2", target_bir_lowering=False, num_devices=1)
    a = {name: np.ascontiguousarray(value) for name, value in inputs.items()}
    columns = [a["L0_xattn_in_proj_b"][0:2 * P]] + [a[name] for name, _ in COLUMNS[1:]]
    rows = [a["L0_xattn_in_proj_b"][2 * P:3 * P]] + [a[name] for name in ROWS[1:]]
    given = {name: a[name] for name in ("x", "ctx_1024", "L0_xattn_in_proj_w", "L0_xattn_out_w", "L1_xattn_W_ff1",
                                        "L1_xattn_W_ff2", "L2_xattn_fc1_w", "L2_xattn_fc2_w", "L3_xattn_ff_w1",
                                        "L3_xattn_ff_w2")}
    given["columns"] = np.concatenate([c.reshape(-1, P) for c in columns])
    given["rows"] = np.stack(rows)[None]
    given["scalars"] = np.concatenate([a[name].reshape(-1) for name in SCALARS])[None]
    given["spread"] = np.concatenate([a[name] for name in SPREAD])[None]
    given["squares"] = np.stack([a[name] for name in SQUARE])
    arrays, ins = {}, {}
    for name, value in given.items():
        arrays[f"in_{name}"] = value
        ins[name] = nc.dram_tensor(f"in_{name}", value.shape, mybir.dt.from_np(value.dtype),
                                   kind="ExternalInput").ap()
    out = nc.dram_tensor("out_0", (B, N, D), F32, kind="ExternalOutput").ap()
    build(nc, ins, out, STOP)
    r = run(nc, [arrays], core_ids=[0])
    return r.results[0]["out_0"]
```
